# Optimizing a Trainium2 kernel written in Bass

```python
import numpy as np
import jax
import jax.numpy as jnp

def _softmax(x, axis=-1):
    return jax.nn.softmax(x, axis=axis)

def _gelu(x):
    return jax.nn.gelu(x, approximate=True)

def _silu(x):
    return jax.nn.silu(x)

def _sigmoid(x):
    return jax.nn.sigmoid(x)

def _layernorm(x, axis=-1, eps=1e-05):
    m = jnp.mean(x, axis=axis, keepdims=True)
    v = jnp.var(x, axis=axis, keepdims=True)
    return (x - m) / jnp.sqrt(v + eps)

def _scatter_add(tgt, idx, src, axis=0):
    return tgt.at[idx].add(src)

def _segment_sum(src, seg, n):
    return jax.ops.segment_sum(src, seg, n)
kernel_name = 'mk_flamingo_gated_d1_seqx_r8_33a254'

def setup_inputs(seed: int=0):
    np.random.seed(seed)
    _w = jnp.asarray

    def _rec_inputs():
        import jax
        import jax.numpy as jnp
        _rk = jax.random.key(seed)
        x = 0.0003765 + 1 * jax.random.normal(jax.random.fold_in(_rk, 1), (16, 128, 256), jnp.float32)
        _lenS = 128 - jax.random.randint(jax.random.fold_in(_rk, 7), (16,), 0, max(1, 128 // 4) + 1, jnp.int32)
        _lenS2 = 128 - jax.random.randint(jax.random.fold_in(_rk, 8), (16,), 0, max(1, 128 // 4) + 1, jnp.int32)
        _ctx_2048P = jax.random.normal(jax.random.fold_in(_rk, 11), (16, 16, 256), jnp.float32)
        _ctx_2048c = jax.random.dirichlet(jax.random.fold_in(_rk, 511), 0.3 * jnp.ones((16,), jnp.float32), (16, 128))
        _ctx_2048t = jnp.einsum('bsk,bkd->bsd', _ctx_2048c, _ctx_2048P)
        _ctx_2048t = _ctx_2048t * jax.lax.rsqrt(jnp.mean(jnp.square(_ctx_2048t)) + 1e-12) * 0.953939
        ctx_2048 = -0.000292821 + 1.00034 * (_ctx_2048t + 0.3 * jax.random.normal(jax.random.fold_in(_rk, 611), (16, 128, 256), jnp.float32))
        _g = jax.random.normal(jax.random.fold_in(_rk, 9001), (2, 1), jnp.float32)
        _g = jnp.sign(_g) * jnp.maximum(jnp.abs(_g), 1.0) + (_g == 0) * 1.0
        g_xattn = _g[0]
        g_ffn = _g[1]
        return (x, ctx_2048, g_xattn, g_ffn)
    x, ctx_2048, g_xattn, g_ffn = _rec_inputs()

    def _L0_xattn_setup():
        import jax, jax.numpy as jnp
        import numpy as np
        key = jax.random.key(seed)
        k1, k2, k3, k4, k5 = jax.random.split(key, 5)
        B, D_MODEL, L = (2, 128, 256)
        HEAD_DIM = 8
        H = D_MODEL // HEAD_DIM
        return {'k': jax.random.normal(k1, (B, D_MODEL, L), dtype=jnp.float32), 'v': jax.random.normal(k2, (B, D_MODEL, L), dtype=jnp.float32), 'q': jax.random.normal(k3, (B, D_MODEL, L), dtype=jnp.float32), 'ssm_kernel': jax.random.normal(k4, (H, L), dtype=jnp.float32), 'D': jax.random.normal(k5, (H,), dtype=jnp.float32), 'head_dim': HEAD_DIM}
    _L0_xattn_all = _L0_xattn_setup()
    _L0_xattn_in = {k: v for k, v in _L0_xattn_all.items() if k in ('ssm_kernel', 'D')}
    del _L0_xattn_all

    def _L0_ffn_setup():
        import jax, jax.numpy as jnp
        import numpy as np
        B, S, D = (4, 256, 256)
        E = 8
        H = 352
        CAP_F = 1.0

        def _moe(x, Wg, W1, W3, W2, sw1, sw3, sw2):
            b, sl, d = x.shape
            T = b * sl
            C = int(CAP_F * T / E)
            xt = x.reshape(T, d)
            probs = jax.nn.softmax(xt @ Wg, axis=-1)
            eidx = jnp.argmax(probs, axis=-1)
            gate = jnp.take_along_axis(probs, eidx[:, None], 1)[:, 0]
            oh = jax.nn.one_hot(eidx, E, dtype=jnp.int32)
            pos = (jnp.cumsum(oh, axis=0) * oh).sum(-1) - 1
            keep = pos < C
            flat = jnp.where(keep, eidx * C + pos, E * C)
            xd = jnp.zeros((E * C, d), x.dtype).at[flat].set(xt, mode='drop')
            xd = xd.reshape(E, C, d)
            h = jax.nn.silu(jnp.einsum('ecd,edh->ech', xd, W1)) * jnp.einsum('ecd,edh->ech', xd, W3)
            oe = jnp.einsum('ech,ehd->ecd', h, W2).reshape(E * C, d)
            out = jnp.take(oe, jnp.minimum(flat, E * C - 1), axis=0)
            out = out * (gate * keep.astype(x.dtype))[:, None]
            shared = jax.nn.silu(xt @ sw1) * (xt @ sw3) @ sw2
            return (out + shared).reshape(b, sl, d)
        key = jax.random.key(seed)
        ks = jax.random.split(key, 8)
        s = lambda fan: 1.0 / np.sqrt(fan)
        return {'x': jax.random.normal(ks[0], (B, S, D), jnp.float32), 'Wg': jax.random.normal(ks[1], (D, E), jnp.float32) * s(D), 'W1': jax.random.normal(ks[2], (E, D, H), jnp.float32) * s(D), 'W3': jax.random.normal(ks[3], (E, D, H), jnp.float32) * s(D), 'W2': jax.random.normal(ks[4], (E, H, D), jnp.float32) * s(H), 'sw1': jax.random.normal(ks[5], (D, H), jnp.float32) * s(D), 'sw3': jax.random.normal(ks[6], (D, H), jnp.float32) * s(D), 'sw2': jax.random.normal(ks[7], (H, D), jnp.float32) * s(H)}
    _L0_ffn_all = _L0_ffn_setup()
    _L0_ffn_in = {k: v for k, v in _L0_ffn_all.items() if k in ('Wg', 'W1', 'W3', 'W2', 'sw1', 'sw3', 'sw2')}
    del _L0_ffn_all
    return {'x': x, 'ctx_2048': ctx_2048, 'g_xattn': g_xattn, 'g_ffn': g_ffn, 'L0_xattn_ssm_kernel': _L0_xattn_in['ssm_kernel'], 'L0_xattn_D': _L0_xattn_in['D'], 'L0_ffn_Wg': _L0_ffn_in['Wg'], 'L0_ffn_W1': _L0_ffn_in['W1'], 'L0_ffn_W3': _L0_ffn_in['W3'], 'L0_ffn_W2': _L0_ffn_in['W2'], 'L0_ffn_sw1': _L0_ffn_in['sw1'], 'L0_ffn_sw3': _L0_ffn_in['sw3'], 'L0_ffn_sw2': _L0_ffn_in['sw2']}

def reference(x, ctx_2048, g_xattn, g_ffn, L0_xattn_ssm_kernel, L0_xattn_D, L0_ffn_Wg, L0_ffn_W1, L0_ffn_W3, L0_ffn_W2, L0_ffn_sw1, L0_ffn_sw3, L0_ffn_sw2):
    import jax
    import jax.numpy as jnp

    def _L0_xattn_ref(k, v, q, ssm_kernel, D, head_dim):
        import jax, jax.numpy as jnp
        import numpy as np
        B, HD, L = k.shape
        H = HD // head_dim
        fft_size = 2 * L
        k_ = k.reshape(B, H, head_dim, L)
        v_ = v.reshape(B, H, head_dim, L)
        q_ = q.reshape(B, H, head_dim, L)
        kv = jnp.einsum('bhil,bhjl->bijhl', k_, v_)
        kv_f = jnp.fft.rfft(kv, n=fft_size)
        kernel_f = jnp.fft.rfft(ssm_kernel, n=fft_size)
        y = jnp.fft.irfft(kv_f * kernel_f, n=fft_size)[..., :L]
        out = y + kv * D[None, None, None, :, None]
        out = jnp.einsum('bijhl,bhil->bjhl', out, q_)
        out = jnp.transpose(out, (0, 2, 1, 3)).reshape(B, H * head_dim, L)
        return out.astype(k.dtype)

    def _L0_ffn_ref(x, Wg, W1, W3, W2, sw1, sw3, sw2):
        import jax, jax.numpy as jnp
        import numpy as np
        B, S, D = (4, 256, 256)
        E = 8
        H = 352
        CAP_F = 1.0

        def _moe(x, Wg, W1, W3, W2, sw1, sw3, sw2):
            b, sl, d = x.shape
            T = b * sl
            C = int(CAP_F * T / E)
            xt = x.reshape(T, d)
            probs = jax.nn.softmax(xt @ Wg, axis=-1)
            eidx = jnp.argmax(probs, axis=-1)
            gate = jnp.take_along_axis(probs, eidx[:, None], 1)[:, 0]
            oh = jax.nn.one_hot(eidx, E, dtype=jnp.int32)
            pos = (jnp.cumsum(oh, axis=0) * oh).sum(-1) - 1
            keep = pos < C
            flat = jnp.where(keep, eidx * C + pos, E * C)
            xd = jnp.zeros((E * C, d), x.dtype).at[flat].set(xt, mode='drop')
            xd = xd.reshape(E, C, d)
            h = jax.nn.silu(jnp.einsum('ecd,edh->ech', xd, W1)) * jnp.einsum('ecd,edh->ech', xd, W3)
            oe = jnp.einsum('ech,ehd->ecd', h, W2).reshape(E * C, d)
            out = jnp.take(oe, jnp.minimum(flat, E * C - 1), axis=0)
            out = out * (gate * keep.astype(x.dtype))[:, None]
            shared = jax.nn.silu(xt @ sw1) * (xt @ sw3) @ sw2
            return (out + shared).reshape(b, sl, d)
        return _moe(x, Wg, W1, W3, W2, sw1, sw3, sw2)
    x = x + jnp.tanh(g_xattn[0]) * _L0_xattn_ref(ctx_2048, ctx_2048, _layernorm(x, axis=-1), L0_xattn_ssm_kernel, L0_xattn_D, 8)
    x = x + jnp.tanh(g_ffn[0]) * _L0_ffn_ref(_layernorm(x, axis=-1), L0_ffn_Wg, L0_ffn_W1, L0_ffn_W3, L0_ffn_W2, L0_ffn_sw1, L0_ffn_sw3, L0_ffn_sw2)
    return x

_drawn_inputs = setup_inputs


def setup_inputs(seed=0):
    import zlib

    import numpy as np

    out = dict(_drawn_inputs(seed))
    spreads = {}
    factors = {'L0_ffn_Wg': 8.0,
     'L0_ffn_W1': 8.0,
     'L0_ffn_W3': 7.643,
     'L0_ffn_W2': 7.608,
     'L0_ffn_sw1': 3.055,
     'L0_ffn_sw3': 2.849,
     'L0_ffn_sw2': 2.859}
    for name, (base, spread) in spreads.items():
        noise = np.random.default_rng([zlib.crc32(name.encode()), seed]).standard_normal(out[name].shape)
        drawn = base * np.exp(spread * noise) if base else spread * noise
        out[name] = jnp.asarray(drawn.astype(out[name].dtype))
    for name, factor in factors.items():
        out[name] = (out[name] * factor).astype(out[name].dtype)
    return out
```

```python
from contextlib import ExitStack

import concourse.bass as bass
from concourse import mybir

F32 = mybir.dt.float32
I32 = mybir.dt.int32
ALU = mybir.AluOpType
ACT = mybir.ActivationFunctionType
AX_X = mybir.AxisListType.X

P = 128
B, CH, L = 16, 128, 256
DH = 8
H = CH // DH
BLK = L // P
NG = 4
GB = B // NG
PL = BLK * GB
NPL = 36
KVH = NPL * PL
QPL = 12
E, HID, CAP = 8, 352, B * CH // 8
KPAD = L + P - 1
HC = [(0, 128), (128, 128), (256, HID - 256)]
ROW = L + 2
EPS = 1e-5
UNITS = H // 2
CONV = NG * UNITS
WRING = 4
XRING, BRING = 3, 3
F0_SLOT = 13
OUT_OF_RANGE = 4096.0


def tail_group(s):
    return s // UNITS - 1, s % UNITS


def transposing_uses():
    uses = [("q", 0, 0), ("q", 0, 1)]
    for s in range(CONV + UNITS):
        g, u = tail_group(s)
        if u == 1 and g >= 0:
            uses += [("r", g, 0), ("r", g, 1)]
        if u == 3 and g >= 0:
            uses += [("xT", g, 0), ("xT", g, 1)]
        if u == 4 and g >= 0:
            uses += [("logits", g, 0)]
        if u == 5 and g + 2 < NG:
            uses += [("q", g + 2, 0), ("q", g + 2, 1)]
        if u == 6 and g >= 0:
            uses += [("pos", g, 0)]
    uses += [("xe", e, 0) for e in range(E)]
    return uses


TP = transposing_uses()
TP_AT = {use: n for n, use in enumerate(TP)}
BY_ACT = {"q": True, "xT": True, "xe": True, "r": False, "logits": False, "pos": False}


def feed_forward_uses():
    uses = []
    for first in (0, 8):
        for n in range(first, first + 8):
            uses += [("gu", n, 0), ("gu", n, 1)]
            if n > first:
                uses += [("y", n - 1, 0)]
            uses += [("gu", n, 2)]
        uses += [("y", first + 7, 0)]
    return uses


FU = feed_forward_uses()
FU_AT = {use: n for n, use in enumerate(FU)}
SHARED_USES = 32
GU_SEQ = [use for use in FU if use[0] == "gu"]
GU_NUM = {use: n for n, use in enumerate(GU_SEQ)}
SLOTS = F0_SLOT + SHARED_USES


def build(nc, x, ctxt, kpad, skip_d, g_x, g_f, wg, w1, w3, w2, sw1, sw3, sw2, out):
    xd = nc.dram_tensor("xd_scratch", (E * CAP, ROW), F32, kind="Internal").ap()
    base = nc.dram_tensor("base_scratch", (B * CH, L), F32, kind="Internal").ap()
    out_rows = out.rearrange("b c l -> (b c) l")

    with ExitStack() as ctx:
        def sb(name, shape, dt=F32):
            return ctx.enter_context(nc.sbuf_tensor(name, shape, dt))

        def sem(name):
            return ctx.enter_context(nc.semaphore(name))

        x_sb = sb("x_sb", [P, B, L])
        ct = sb("ct", [P, NG, H * 64])
        toep = sb("toep", [P, H, L])
        kv = sb("kv", [P, 2, H * KVH])
        qr = sb("qr", [P, 2, H * QPL * PL])
        prod = sb("prod", [P, 2, 2 * 512])
        r_sb = sb("r_sb", [P, 2, H * 64])
        xn = sb("xn", [P, GB, L])
        xrow = sb("xrow", [P, B, ROW])
        xT = sb("xT", [P, 2, 2, GB * P])
        wg_sb = sb("wg_sb", [P, 2, E])
        ws_gu = sb("ws_gu", [P, 2, 2, HID])
        ws_d = sb("ws_d", [P, 3, L])
        we_gu = sb("we_gu", [P, WRING, 2 * 2 * HID])
        we_d = sb("we_d", [P, WRING, 3 * L])
        sg = sb("sg", [P, 2, 256])
        hT = sb("hT", [P, 2, 3, 256])
        stats = sb("stats", [P, GB, 6])
        mv = sb("mv", [P, GB, 2])
        veps = sb("veps", [P, GB])
        mneg = sb("mneg", [P, GB])
        rstd = sb("rstd", [P, GB])
        nbias = sb("nbias", [P, GB])
        mhalf = sb("mhalf", [P, GB])
        econst = sb("econst", [P, GB * E])
        ident = sb("ident", [P, P])
        anti = sb("anti", [P, P])
        tri = sb("tri", [P, P])
        ones = sb("ones", [P, P])
        zeros = sb("zeros", [P, 4 * ROW])
        d_bc = sb("d_bc", [P, H])
        gates = sb("gates", [P, 2])
        tg = sb("tg", [P, 2])
        ebase = sb("ebase", [P, GB, E])
        prio = sb("prio", [P, GB, E])
        mx = sb("mx", [P, GB])
        sh = sb("sh", [P, GB, E])
        ex = sb("ex", [P, GB, E])
        se = sb("se", [P, GB])
        gp = sb("gp", [P, GB])
        eq = sb("eq", [P, GB, E])
        ms = sb("ms", [P, GB])
        oh = sb("oh", [P, B, E])
        acc = sb("acc", [P, B + 1, E])
        t1 = sb("t1", [P, GB, E])
        t2 = sb("t2", [P, GB, E])
        t3 = sb("t3", [P, GB, E])
        slotf = sb("slotf", [P, GB])
        dest = sb("dest", [P, B], I32)
        after, o = kv[:, 0, :], 0
        xe = after[:, o:o + XRING * 2 * ROW].rearrange("p (i t n) -> p i t n", i=XRING, t=2)
        o += XRING * 2 * ROW
        bg = after[:, o:o + BRING * 2 * L].rearrange("p (i t n) -> p i t n", i=BRING, t=2)
        o += BRING * 2 * L
        fin = after[:, o:o + 4 * L].rearrange("p (i t n) -> p i t n", i=2, t=2)
        xeT = kv[:, 1, 0:4 * CAP].rearrange("p (i n) -> p i n", i=2)
        tok = sb("tok", [P, E, 2], I32)
        tv = sb("tv", [P, 2])

        z = [ctx.enter_context(nc.psum_tensor(f"z{i}", [P, 2, 512], F32)) for i in range(2)]
        fb = [ctx.enter_context(nc.psum_tensor(f"fb{i}", [P, 512], F32)) for i in range(2)]
        tp = [ctx.enter_context(nc.psum_tensor(f"tp{i}", [P, 512], F32)) for i in range(2)]

        x_in = [sem(f"x_in{g}") for g in range(NG)]
        ctx_in = [sem(f"ctx_in{g}") for g in range(NG)]
        toep_in = [sem(f"toep_in{k}") for k in range(4)]
        small_in = sem("small_in")
        shared_in = sem("shared_in")
        expert_in = [sem(f"expert_in{e}") for e in range(E)]
        xd_zeroed = sem("xd_zeroed")
        pool_consts = sem("pool_consts")
        dve_consts = sem("dve_consts")
        tanh_done = sem("tanh_done")
        diag_added = sem("diag_added")
        kv_pool = sem("kv_pool")
        kv_dve = sem("kv_dve")
        stats_done = sem("stats_done")
        rstd_done = sem("rstd_done")
        xn_done = sem("xn_done")
        xrow_done = sem("xrow_done")
        q_done = sem("q_done")
        z_ready = sem("z_ready")
        prods = sem("prods")
        reduced = sem("reduced")
        tp_ready = sem("tp_ready")
        tp_free_act = sem("tp_free_act")
        tp_free_dve = sem("tp_free_dve")
        f_ready = sem("f_ready")
        silu_done = sem("silu_done")
        f_free = sem("f_free")
        shifted = sem("shifted")
        exp_done = sem("exp_done")
        onehot = sem("onehot")
        gate_done = sem("gate_done")
        dest_done = sem("dest_done")
        link = sem("link")
        plink = sem("plink")
        scattered = sem("scattered")
        base_stored = sem("base_stored")
        xe_in = [sem(f"xe_in{i}") for i in range(XRING)]
        tok_done = sem("tok_done")
        gathered = [sem(f"gathered{i}") for i in range(BRING)]
        stored = [sem(f"stored{i}") for i in range(2)]

        def view(t, off, dims, parts=P):
            a = t[:]
            row = a.ap[0][0]
            return bass.AP(a.tensor, a.offset + off, [[row, parts], *dims])

        def tp_wait(eng, n):
            if n >= 2:
                by_act = BY_ACT[TP[n - 2][0]]
                count = sum(BY_ACT[TP[k][0]] == by_act for k in range(n - 1))
                eng.wait_ge(tp_free_act if by_act else tp_free_dve, count)

        def f_bank(n):
            if n < SHARED_USES:
                return fb[n % 2][:, :], n - 2
            m = n - SHARED_USES
            k = m % 6
            bank = fb[k][:, :] if k < 2 else z[(k - 2) // 2][:, k % 2, :]
            if m < 2:
                return bank, n - 2
            return bank, (n - 6 if m >= 6 else None)

        def weights(n):
            if n < 8:
                gu = lambda m, k, c, w: ws_gu[:, m, k, c:c + w]
                down = lambda c, w: ws_d[0:w, c, :]
            else:
                q = (n - 8) % WRING
                gu = lambda m, k, c, w: we_gu[:, q, (m * 2 + k) * HID + c:(m * 2 + k) * HID + c + w]
                down = lambda c, w: we_d[0:w, q, c * L:(c + 1) * L]
            return gu, down

        norms = [("ln1", 0)]
        for s in range(CONV + UNITS):
            g, u = tail_group(s)
            if u == 1 and g >= 0:
                norms.append(("ln2", g))
            if u == 2 and g + 2 < NG:
                norms.append(("ln1", g + 2))
        NORM_AT = {what: n for n, what in enumerate(norms)}

        def norm_read(eng, n):
            what, g = norms[n]
            eng.wait_ge(xn_done if what == "ln1" else xrow_done, g + 1)

        def load_rows(sp, e):
            if e == 0:
                sp.wait_ge(scattered, 16 * B)
            if e >= XRING:
                sp.wait_ge(tp_ready, TP_AT[("xe", e - XRING, 0)] + 1)
                sp.wait_ge(tok_done, e - XRING + 1)
                sp.wait_ge(f_free, FU_AT[("y", 8 + e - XRING, 0)] + 1)
            sp.dma_start(xe[:, e % XRING, :, :],
                         xd[e * CAP:(e + 1) * CAP, :].rearrange("(t p) n -> p t n", p=P)).then_inc(xe_in[e % XRING], 16)

        def kv_products(eng, g, c, done):
            kvg, cg = (kv, (g % 2) * H * KVH + 4 * c * KVH), (ct, g * H * 64 + 4 * c * 64)

            def mul(o, a, b, n):
                return eng.tensor_tensor(view(kvg[0], kvg[1] + o, [[KVH, 4], [1, n]]),
                                         view(cg[0], cg[1] + a, [[64, 4], [1, n]]),
                                         view(cg[0], cg[1] + b, [[64, 4], [1, n]]), ALU.mult)
            mul(0, 0, 0, 64)
            for d in range(1, 4):
                mul(64 * d, 0, 8 * d, 8 * (8 - d))
                mul(64 * d + 8 * (8 - d), 8 * (8 - d), 0, 8 * d)
            mul(256, 0, 32, 32).then_inc(done, 1)

        block = ctx.enter_context(nc.Block())

        @block.sync
        def _(sp):
            def load_group(g):
                sp.dma_start(ct[:, g, :], ctxt[g]).then_inc(ctx_in[g], 16)
                sp.dma_start(x_sb[:, GB * g:GB * (g + 1), :],
                             x[GB * g:GB * (g + 1)].rearrange("b c l -> c b l")).then_inc(x_in[g], 16)

            def load_toeplitz(k):
                src = bass.AP(kpad.tensor, kpad.offset + 4 * k * KPAD, [[1, P], [KPAD, 4], [1, L]])
                sp.dma_start(toep[:, 4 * k:4 * k + 4, :], src).then_inc(toep_in[k], 16)

            def load_ffn(gu, down, a1, a3, a2, s):
                for m, a in ((0, a1), (1, a3)):
                    sp.dma_start(gu[m], a.rearrange("(k p) n -> p k n", p=P)).then_inc(s, 16)
                sp.dma_start(down(slice(0, P), 0, 2), a2[0:256, :].rearrange("(k p) n -> p k n", p=P)).then_inc(s, 16)
                sp.dma_start(down(slice(0, HC[2][1]), 2, 3),
                             a2[256:HID, :].rearrange("(k p) n -> p k n", k=1)).then_inc(s, 16)

            def load_expert(e):
                q = e % WRING
                if e >= WRING:
                    sp.wait_ge(f_ready, FU_AT[("y", 8 + e - WRING, 0)] + 1)
                gu = [we_gu[:, q, m * 2 * HID:(m + 1) * 2 * HID].rearrange("p (k n) -> p k n", k=2) for m in range(2)]
                wd = we_d[:, q, :].rearrange("p (k n) -> p k n", k=3)
                load_ffn(gu, lambda p, a, b: wd[p, a:b, :], w1[e], w3[e], w2[e], expert_in[e])

            sp.dma_start(ct[:, 0, :], ctxt[0]).then_inc(ctx_in[0], 16)
            sp.dma_start(x_sb[:, 0:GB, :], x[0:GB].rearrange("b c l -> c b l")).then_inc(x_in[0], 16)
            sp.dma_start(d_bc[:, :], bass.AP(skip_d.tensor, skip_d.offset, [[0, P], [1, H]])).then_inc(small_in, 16)
            sp.dma_start(gates[:, 0:1], bass.AP(g_x.tensor, g_x.offset, [[0, P], [1, 1]])).then_inc(small_in, 16)
            sp.dma_start(gates[:, 1:2], bass.AP(g_f.tensor, g_f.offset, [[0, P], [1, 1]])).then_inc(small_in, 16)
            sp.dma_start(wg_sb[:, :, :], wg.rearrange("(k p) e -> p k e", p=P)).then_inc(small_in, 16)
            for k in range(4):
                load_toeplitz(k)
            sp.wait_ge(dve_consts, 4)
            xd_flat = xd.rearrange("(p q r) n -> q p (r n)", p=P, q=4)
            for k in range(4):
                sp.dma_start(xd_flat[k], zeros[:, :]).then_inc(xd_zeroed, 16)
            for g in range(1, NG):
                load_group(g)
                if g == 1:
                    load_ffn([ws_gu[:, m, :, :] for m in range(2)], lambda p, a, b: ws_d[p, a:b, :],
                             sw1, sw3, sw2, shared_in)
            for e in range(WRING):
                load_expert(e)
            for n in range(8):
                sp.wait_ge(f_free, FU_AT[("y", n, 0)] + 1)
                for dst in (out, base.rearrange("(b c) l -> b c l", c=CH)):
                    sp.dma_start(dst[2 * n:2 * n + 2].rearrange("b c l -> c b l"),
                                 x_sb[:, 2 * n:2 * n + 2, :]).then_inc(base_stored, 16)
                if n == 6:
                    for e in range(2):
                        load_rows(sp, e)
            for e in range(2, E):
                load_rows(sp, e)
                if e - 2 + WRING < E:
                    load_expert(e - 2 + WRING)
            for i in range(2):
                sp.wait_ge(stored[i], 16 * 2 * (E // 2))

        @block.gpsimd
        def _(pool):
            linked = [0]

            def chain(ins):
                linked[0] += 1
                ins.then_inc(plink, 1)
                pool.wait_ge(plink, linked[0])

            def scale_and_bias(n):
                pool.wait_ge(stats_done, n + 1)
                if n >= 1:
                    norm_read(pool, n - 1)
                chain(pool.tensor_tensor(rstd[:, :], veps[:, :], mhalf[:, :], ALU.pow))
                pool.tensor_tensor(nbias[:, :], mneg[:, :], rstd[:, :], ALU.mult).then_inc(rstd_done, 1)

            chain(pool.memset(ident[:, :], 0.0))
            pool.affine_select(out=ident[:, :], in_=ident[:, :], compare_op=ALU.not_equal, fill=1.0, base=0,
                               pattern=[[-1, P]], channel_multiplier=1).then_inc(pool_consts, 1)
            chain(pool.memset(anti[:, :], 0.0))
            pool.affine_select(out=anti[:, :], in_=anti[:, :], compare_op=ALU.not_equal, fill=1.0, base=1 - P,
                               pattern=[[1, P]], channel_multiplier=1).then_inc(pool_consts, 1)
            pool.wait_ge(dve_consts, 4)
            scale_and_bias(0)
            pool.wait_ge(ctx_in[0], 16)
            for c in range(1, 4):
                kv_products(pool, 0, c, kv_pool)
            pool.affine_select(out=tri[:, :], in_=ones[:, :], compare_op=ALU.is_ge, fill=0.0, base=-1,
                               pattern=[[1, P]], channel_multiplier=-1).then_inc(pool_consts, 1)
            pool.iota(ebase[:, :, :], pattern=[[0, GB], [CAP, E]], base=0, channel_multiplier=0,
                      allow_small_or_imprecise_dtypes=True).then_inc(pool_consts, 1)
            pool.iota(prio[:, :, :], pattern=[[0, GB], [-1, E]], base=E, channel_multiplier=0,
                      allow_small_or_imprecise_dtypes=True).then_inc(pool_consts, 1)
            pool.iota(xrow[:, :, L + 1:L + 2], pattern=[[P, B], [1, 1]], base=1, channel_multiplier=1,
                      allow_small_or_imprecise_dtypes=True).then_inc(pool_consts, 1)
            for s in range(CONV + UNITS):
                g, u = tail_group(s)
                if u % 2 == 0 and g + 2 < NG:
                    if u == 0:
                        pool.wait_ge(ctx_in[g + 2], 16)
                        if g >= 0:
                            pool.wait_ge(z_ready, UNITS * (g + 1))
                    kv_products(pool, g + 2, u // 2, kv_pool)
                if s == CONV:
                    pool.wait_ge(z_ready, CONV)
                    pool.memset(bg[:, :, :, :], 0.0).then_inc(pool_consts, 1)
                if u == 1 and g >= 0:
                    scale_and_bias(NORM_AT[("ln2", g)])
                if u == 2 and g + 2 < NG:
                    scale_and_bias(NORM_AT[("ln1", g + 2)])
                if u == 4 and g >= 0:
                    pool.wait_ge(shifted, g + 1)
                    if g >= 1:
                        pool.wait_ge(gate_done, g)
                    pool.tensor_tensor(ex[:, :, :].rearrange("p b e -> p (b e)"), econst[:, :],
                                       sh[:, :, :].rearrange("p b e -> p (b e)"), ALU.pow).then_inc(exp_done, 1)
                if u == 6 and g >= 0:
                    if g == 0:
                        pool.wait_ge(xd_zeroed, 16 * 4)
                        pool.wait_ge(pool_consts, 6)
                    pool.wait_ge(dest_done, g + 1)
                    pool.wait_ge(gate_done, g + 1)
                    for b in range(GB * g, GB * (g + 1)):
                        pool.indirect_dma_start(
                            out=xd, out_offset=bass.IndirectOffsetOnAxis(ap=dest[:, b:b + 1], axis=0),
                            in_=xrow[:, b, :], in_offset=None, bounds_check=E * CAP - 1,
                            oob_is_err=False).then_inc(scattered, 16)

            def gather(e):
                pool.wait_ge(tok_done, e + 1)
                if e == 0:
                    pool.wait_ge(base_stored, 16 * 16)
                    pool.wait_ge(pool_consts, 7)
                if e >= BRING:
                    pool.wait_ge(f_free, FU_AT[("y", 8 + e - BRING, 0)] + 1)
                for t in range(2):
                    pool.indirect_dma_start(
                        out=bg[:, e % BRING, t, :], out_offset=None, in_=base,
                        in_offset=bass.IndirectOffsetOnAxis(ap=tok[:, e, t:t + 1], axis=0),
                        bounds_check=B * CH - 1, oob_is_err=False).then_inc(gathered[e % BRING], 16)

            gather(0)
            for e in range(E):
                if e + 1 < E:
                    gather(e + 1)
                pool.wait_ge(f_free, FU_AT[("y", 8 + e, 0)] + 1)
                for t in range(2):
                    pool.indirect_dma_start(
                        out=out_rows, out_offset=bass.IndirectOffsetOnAxis(ap=tok[:, e, t:t + 1], axis=0),
                        in_=fin[:, e % 2, t, :], in_offset=None, bounds_check=B * CH - 1,
                        oob_is_err=False).then_inc(stored[e % 2], 16)

        @block.scalar
        def _(act):
            def normalise(n, dst, free):
                what, g = norms[n]
                act.wait_ge(rstd_done, n + 1)
                free()
                for b in range(GB):
                    last = act.activation(dst(b), x_sb[:, GB * g + b, :], ACT.Identity,
                                          bias=nbias[:, b:b + 1], scale=rstd[:, b:b + 1])
                last.then_inc(xn_done if what == "ln1" else xrow_done, 1)

            def norm1(g):
                def free():
                    if g >= 1:
                        act.wait_ge(tp_ready, TP_AT[("q", g - 1, 1)] + 1)
                normalise(NORM_AT[("ln1", g)], lambda b: xn[:, b, :], free)

            def norm2(g):
                normalise(NORM_AT[("ln2", g)], lambda b: xrow[:, GB * g + b, 0:L], lambda: None)

            def q_copy(g):
                o = (g % 2) * H * QPL * PL
                if g >= 2:
                    act.wait_ge(prods, UNITS * (g - 1))
                for k in range(BLK):
                    n = TP_AT[("q", g, k)]
                    act.wait_ge(tp_ready, n + 1)
                    act.activation(view(qr, o + GB * k, [[QPL * PL, H], [PL, DH], [1, GB]]),
                                   view(tp[n % 2], 0, [[DH, H], [1, DH], [P, GB]]),
                                   ACT.Copy).then_inc(tp_free_act, 1)
                act.wait_ge(tp_free_act, sum(BY_ACT[k[0]] for k in TP[:TP_AT[("q", g, 1)] + 1]))
                act.activation(view(qr, o + DH * PL, [[QPL * PL, H], [1, 4 * PL]]),
                               view(qr, o, [[QPL * PL, H], [1, 4 * PL]]), ACT.Copy).then_inc(q_done, 1)

            def xT_copy(g):
                if g >= 2:
                    act.wait_ge(f_ready, FU_AT[("gu", 2 * (g - 2) + 1, 2)] + 1)
                for k in range(2):
                    n = TP_AT[("xT", g, k)]
                    act.wait_ge(tp_ready, n + 1)
                    act.activation(xT[:, g % 2, k, :], tp[n % 2][:, :], ACT.Copy).then_inc(tp_free_act, 1)

            def silu(n):
                kind, blk, c = FU[n]
                if kind != "gu":
                    return
                k = GU_NUM[FU[n]]
                act.wait_ge(f_ready, n + 1)
                if k >= 2:
                    act.wait_ge(f_free, FU_AT[GU_SEQ[k - 2]] + 1)
                bank, _ = f_bank(n)
                act.activation(sg[0:HC[c][1], k % 2, :], bank[0:HC[c][1], 0:256], ACT.Silu).then_inc(silu_done, 1)

            def xeT_copy(e):
                n = TP_AT[("xe", e, 0)]
                act.wait_ge(tp_ready, n + 1)
                if e >= 2:
                    act.wait_ge(f_ready, FU_AT[("gu", 8 + e - 2, 2)] + 1)
                act.activation(xeT[:, e % 2, :], tp[n % 2][:, :], ACT.Copy).then_inc(tp_free_act, 1)

            act.wait_ge(small_in, 16 * 4)
            act.activation(tg[:, :], gates[:, :], ACT.Tanh).then_inc(tanh_done, 1)
            norm1(0)
            q_copy(0)
            for s in range(SLOTS):
                g, u = tail_group(s)
                if g < NG:
                    if u == 2 and g >= 0:
                        norm2(g)
                    if u == 3 and g >= 0:
                        xT_copy(g)
                    if u == 4 and g + 2 < NG:
                        norm1(g + 2)
                    if u == 5 and g + 2 < NG:
                        q_copy(g + 2)
                if s >= F0_SLOT:
                    silu(s - F0_SLOT)
            xeT_copy(0)
            for n in range(SHARED_USES, len(FU)):
                kind, blk, c = FU[n]
                silu(n)
                if kind == "gu" and c == 1 and blk + 1 < 16:
                    xeT_copy(blk + 1 - 8)

        @block.vector
        def _(dve):
            linked = [0]

            def chain(ins):
                linked[0] += 1
                ins.then_inc(link, 1)
                dve.wait_ge(link, linked[0])

            def norm_stats(n):
                what, g = norms[n]
                if n >= 1:
                    dve.wait_ge(rstd_done, n)
                for b in range(GB):
                    ins = dve.bn_stats(stats[:, b, :], x_sb[:, GB * g + b, :])
                chain(ins)
                for b in range(GB):
                    ins = dve.bn_aggr(mv[:, b, :], stats[:, b, :])
                chain(ins)
                dve.tensor_scalar(veps[:, :], mv[:, :, 1], EPS, None, ALU.add)
                dve.tensor_scalar(mneg[:, :], mv[:, :, 0], -1.0, None, ALU.mult).then_inc(stats_done, 1)

            def products(s):
                g, u = divmod(s, UNITS)
                dve.wait_ge(z_ready, s + 1)
                dve.wait_ge(q_done, g + 1)
                if s >= 2:
                    dve.wait_ge(reduced, s - 1)
                q0 = (g % 2) * H * QPL * PL + 2 * u * QPL * PL
                p0 = (s % 2) * 1024
                zt = z[s % 2]

                def mul(o, zo, qo, od, zd, qd):
                    return dve.tensor_tensor(view(prod, p0 + o, [[512, 2], *od]), view(zt, zo, [[512, 2], *zd]),
                                             view(qr, q0 + qo, [[QPL * PL, 2], *qd]), ALU.mult)
                mul(0, 0, 0, [[64, 4], [1, 64]], [[64, 4], [1, 64]], [[PL, 4], [1, 64]])
                mul(256, 256, 32, [[32, 2], [1, 32]], [[0, 2], [1, 32]], [[32, 2], [1, 32]])
                mul(320 + 8, 64, 0, [[72, 2], [1, 64]], [[64, 2], [1, 64]], [[0, 2], [1, 64]])
                mul(448 + 24, 192, 0, [[1, 40]], [[1, 40]], [[1, 40]])
                mul(320, 192 + 40, 40, [[72, 3], [1, 8]], [[8, 3], [1, 8]], [[8, 3], [1, 8]]).then_inc(prods, 1)

            def add_terms(s):
                g, u = divmod(s, UNITS)
                dve.wait_ge(prods, s + 1)
                if g >= 2 and u == 0:
                    dve.wait_ge(tp_ready, TP_AT[("r", g - 2, 1)] + 1)
                o = (g % 2) * H * 64 + 2 * u * 64
                dve.tensor_reduce(view(r_sb, o, [[64, 2], [1, 64]]),
                                  view(prod, (s % 2) * 1024, [[512, 2], [1, 64], [64, 8]]),
                                  AX_X, ALU.add).then_inc(reduced, 1)

            def first_residual(g):
                for k in range(2):
                    n = TP_AT[("r", g, k)]
                    dve.wait_ge(tp_ready, n + 1)
                    if g == 0 and k == 0:
                        dve.wait_ge(tanh_done, 1)
                    xb = x_sb[:, GB * g + 2 * k:GB * g + 2 * k + 2, :].rearrange("p b l -> p (b l)")
                    ins = dve.scalar_tensor_tensor(out=xb, in0=tp[n % 2][:, :], scalar=tg[:, 0:1], in1=xb,
                                                   op0=ALU.mult, op1=ALU.add)
                    ins.then_inc(tp_free_dve, 1)
                dve.wait_ge(tp_free_dve, sum(not BY_ACT[k[0]] for k in TP[:n + 1]))

            def bcast(t):
                return view(t, 0, [[1, GB], [0, E]])

            def choose(g):
                n = TP_AT[("logits", g, 0)]
                lg = view(tp[n % 2], 0, [[E, GB], [1, E]])
                dve.wait_ge(tp_ready, n + 1)
                if g == 0:
                    dve.wait_ge(pool_consts, 6)
                if g >= 1:
                    dve.wait_ge(exp_done, g)
                chain(dve.tensor_reduce(mx[:, :], lg, AX_X, ALU.max))
                dve.tensor_tensor(sh[:, :, :], lg, bcast(mx), ALU.subtract).then_inc(shifted, 1)
                dve.wait_ge(shifted, g + 1)
                dve.tensor_scalar(eq[:, :, :], sh[:, :, :], 0.0, None, ALU.is_equal).then_inc(tp_free_dve, 1)
                dve.wait_ge(tp_free_dve, sum(not BY_ACT[k[0]] for k in TP[:n + 1]))
                chain(dve.tensor_tensor(t1[:, :, :], eq[:, :, :], prio[:, :, :], ALU.mult))
                chain(dve.tensor_reduce(ms[:, :], t1[:, :, :], AX_X, ALU.max))
                o = oh[:, GB * g:GB * (g + 1), :]
                chain(dve.tensor_tensor(o, t1[:, :, :], bcast(ms), ALU.is_equal))
                for b in range(GB * g, GB * (g + 1)):
                    ins = dve.tensor_tensor(acc[:, b + 1, :], acc[:, b, :], oh[:, b, :], ALU.add)
                    if b < GB * (g + 1) - 1:
                        chain(ins)
                ins.then_inc(onehot, 1)
                dve.wait_ge(onehot, g + 1)

            def gate(g):
                dve.wait_ge(exp_done, g + 1)
                chain(dve.tensor_reduce(se[:, :], ex[:, :, :], AX_X, ALU.add))
                chain(dve.reciprocal(gp[:, :], se[:, :]))
                dve.tensor_scalar(xrow[:, GB * g:GB * (g + 1), L], gp[:, :], tg[:, 1:2], None,
                                  ALU.mult).then_inc(gate_done, 1)

            def slot_of_token(g):
                n = TP_AT[("pos", g, 0)]
                pos = view(tp[n % 2], 0, [[E, GB], [1, E]])
                dve.wait_ge(tp_ready, n + 1)
                chain(dve.tensor_scalar(t1[:, :, :], pos, float(CAP), OUT_OF_RANGE, ALU.is_ge, ALU.mult))
                ins = dve.tensor_tensor(t2[:, :, :], pos, t1[:, :, :], ALU.add)
                ins.then_inc(tp_free_dve, 1)
                dve.wait_ge(tp_free_dve, sum(not BY_ACT[k[0]] for k in TP[:n + 1]))
                chain(dve.tensor_tensor(t3[:, :, :], t2[:, :, :], ebase[:, :, :], ALU.add))
                chain(dve.tensor_tensor(t2[:, :, :], t3[:, :, :], oh[:, GB * g:GB * (g + 1), :], ALU.mult))
                chain(dve.tensor_reduce(slotf[:, :], t2[:, :, :], AX_X, ALU.add))
                dve.tensor_copy(dest[:, GB * g:GB * (g + 1)], slotf[:, :]).then_inc(dest_done, 1)

            def feed_forward(n):
                kind, blk, c = FU[n]
                bank, _ = f_bank(n)
                if kind == "gu":
                    w = HC[c][1]
                    k = GU_NUM[FU[n]]
                    dve.wait_ge(silu_done, k + 1)
                    if blk >= 2 and c == 0:
                        dve.wait_ge(f_ready, FU_AT[("y", blk - 2, 0)] + 1)
                    dve.tensor_tensor(hT[0:w, blk % 2, c, :], bank[0:w, 256:512], sg[0:w, k % 2, :],
                                      ALU.mult).then_inc(f_free, 1)
                elif blk < 8:
                    dve.wait_ge(f_ready, n + 1)
                    xb = x_sb[:, 2 * blk:2 * blk + 2, :].rearrange("p b l -> p (b l)")
                    dve.scalar_tensor_tensor(out=xb, in0=bank, scalar=tg[:, 1:2], in1=xb,
                                             op0=ALU.mult, op1=ALU.add).then_inc(f_free, 1)
                else:
                    e = blk - 8
                    dve.wait_ge(f_ready, n + 1)
                    dve.wait_ge(gathered[e % BRING], 32 * (e // BRING + 1))
                    if e >= 2:
                        dve.wait_ge(stored[e % 2], 32 * (e // 2))
                    for t in range(2):
                        ins = dve.scalar_tensor_tensor(
                            out=fin[:, e % 2, t, :], in0=bank[:, t * L:(t + 1) * L],
                            scalar=xe[:, e % XRING, t, L:L + 1], in1=bg[:, e % BRING, t, :],
                            op0=ALU.mult, op1=ALU.add)
                    ins.then_inc(f_free, 1)

            def tokens_of_slots(e):
                dve.wait_ge(xe_in[e % XRING], 16 * (e // XRING + 1))
                v = xe[:, e % XRING, :, L + 1]
                chain(dve.tensor_scalar(tv[:, :], v, 0.0, OUT_OF_RANGE, ALU.is_equal, ALU.mult))
                ins = dve.scalar_tensor_tensor(out=tok[:, e, :], in0=tv[:, :], scalar=-1.0, in1=v,
                                               op0=ALU.add, op1=ALU.add)
                ins.then_inc(tok_done, 1)
                dve.wait_ge(tok_done, e + 1)

            dve.memset(mhalf[:, :], -0.5).then_inc(dve_consts, 1)
            dve.memset(econst[:, :], 2.718281828459045).then_inc(dve_consts, 1)
            dve.memset(ones[:, :], 1.0).then_inc(dve_consts, 1)
            dve.memset(zeros[:, :], 0.0).then_inc(dve_consts, 1)
            dve.memset(acc[:, 0, :], 0.0).then_inc(dve_consts, 1)
            dve.wait_ge(dve_consts, 5)
            dve.wait_ge(x_in[0], 16)
            norm_stats(0)
            dve.wait_ge(ctx_in[0], 16)
            kv_products(dve, 0, 0, kv_dve)
            dve.wait_ge(small_in, 16 * 4)
            dve.wait_ge(pool_consts, 2)
            for h in range(H):
                if h % 4 == 0:
                    dve.wait_ge(toep_in[h // 4], 16)
                dve.scalar_tensor_tensor(out=toep[:, h, 0:P], in0=anti[:, :], scalar=d_bc[:, h:h + 1],
                                         in1=toep[:, h, 0:P], op0=ALU.mult, op1=ALU.add).then_inc(diag_added, 1)
            for s in range(SLOTS):
                g, u = tail_group(s)
                if s < CONV:
                    products(s)
                if 1 <= s <= CONV:
                    add_terms(s - 1)
                if g < NG:
                    if u == 1 and g >= 0:
                        first_residual(g)
                        norm_stats(NORM_AT[("ln2", g)])
                    if u == 2 and g + 2 < NG:
                        dve.wait_ge(x_in[g + 2], 16)
                        norm_stats(NORM_AT[("ln1", g + 2)])
                    if u == 4 and g >= 0:
                        choose(g)
                    if u == 5 and g >= 0:
                        gate(g)
                    if u == 6 and g >= 0:
                        slot_of_token(g)
                if s >= F0_SLOT:
                    feed_forward(s - F0_SLOT)
            tokens_of_slots(0)
            for n in range(SHARED_USES, len(FU)):
                kind, blk, c = FU[n]
                feed_forward(n)
                if kind == "gu" and c == 1 and blk + 1 < 16:
                    tokens_of_slots(blk + 1 - 8)

        @block.tensor
        def _(pe):
            def convolve(s):
                g, u = divmod(s, UNITS)
                c = u // 2
                if g == 0 and c == 0:
                    pe.wait_ge(kv_dve, 1)
                else:
                    pe.wait_ge(kv_pool, 4 * g + c)
                if g == 0:
                    pe.wait_ge(diag_added, 2 * u + 2)
                if s >= 2:
                    pe.wait_ge(prods, s - 1)
                for k in range(2):
                    h = 2 * u + k
                    o = (g % 2) * H * KVH + h * KVH
                    pe.matmul(view(z[s % 2], k * 512 + GB, [[PL, NPL], [1, GB]]), toep[:, h, P:2 * P],
                              view(kv, o, [[PL, NPL], [1, GB]]), start=True, stop=False,
                              skip_group_check=True)
                    mm = pe.matmul(z[s % 2][:, k, 0:KVH], toep[:, h, 0:P], view(kv, o, [[1, KVH]]),
                                   start=False, stop=True, skip_group_check=True)
                mm.then_inc(z_ready, 1)

            def turn_q(g):
                pe.wait_ge(xn_done, g + 1)
                for k in range(BLK):
                    n = TP_AT[("q", g, k)]
                    tp_wait(pe, n)
                    for b in range(GB):
                        mm = pe.transpose(tp[n % 2][:, b * P:(b + 1) * P], xn[:, b, k * P:(k + 1) * P], ident[:, :])
                    mm.then_inc(tp_ready, 1)

            def turn_r(g):
                pe.wait_ge(reduced, UNITS * (g + 1))
                for k in range(2):
                    n = TP_AT[("r", g, k)]
                    tp_wait(pe, n)
                    for j in range(2 * BLK):
                        b, blk = 2 * k + j // BLK, j % BLK
                        src = view(r_sb, (g % 2) * H * 64 + blk * GB + b, [[PL, CH]])
                        mm = pe.transpose(tp[n % 2][:, j * P:(j + 1) * P], src, ident[:, :])
                    mm.then_inc(tp_ready, 1)

            def turn_xT(g):
                pe.wait_ge(xrow_done, g + 1)
                for k in range(2):
                    n = TP_AT[("xT", g, k)]
                    tp_wait(pe, n)
                    for b in range(GB):
                        mm = pe.transpose(tp[n % 2][:, b * P:(b + 1) * P],
                                          xrow[:, GB * g + b, k * P:(k + 1) * P], ident[:, :])
                    mm.then_inc(tp_ready, 1)

            def wait_xT(g):
                pe.wait_ge(tp_free_act, sum(BY_ACT[k[0]] for k in TP[:TP_AT[("xT", g, 1)] + 1]))

            def logits(g):
                n = TP_AT[("logits", g, 0)]
                tp_wait(pe, n)
                wait_xT(g)
                if g == 0:
                    pe.wait_ge(small_in, 16 * 4)
                for b in range(GB):
                    for k in range(2):
                        mm = pe.matmul(tp[n % 2][:, b * E:(b + 1) * E], xT[:, g % 2, k, b * P:(b + 1) * P],
                                       wg_sb[:, k, :], start=(k == 0), stop=(k == 1))
                mm.then_inc(tp_ready, 1)

            def places(g):
                n = TP_AT[("pos", g, 0)]
                tp_wait(pe, n)
                pe.wait_ge(onehot, g + 1)
                if g == 0:
                    pe.wait_ge(pool_consts, 3)
                o = tp[n % 2][:, 0:GB * E]
                pe.matmul(o, tri[:, :], oh[:, GB * g:GB * (g + 1), :].rearrange("p b e -> p (b e)"),
                          start=True, stop=False)
                pe.matmul(o, ones[:, :], acc[:, GB * g:GB * (g + 1), :].rearrange("p b e -> p (b e)"),
                          start=False, stop=True).then_inc(tp_ready, 1)

            def feed_forward(n):
                kind, blk, c = FU[n]
                bank, before = f_bank(n)
                if before is None:
                    pe.wait_ge(prods, CONV)
                elif before >= 0:
                    pe.wait_ge(f_free, before + 1)
                gu, down = weights(blk)
                if kind == "gu":
                    w = HC[c][1]
                    if c == 0:
                        if blk < 8:
                            wait_xT(blk // 2)
                            if blk == 0:
                                pe.wait_ge(shared_in, 16 * 4)
                        else:
                            pe.wait_ge(expert_in[blk - 8], 16 * 4)
                            pe.wait_ge(tp_free_act, sum(BY_ACT[k[0]] for k in TP[:TP_AT[("xe", blk - 8, 0)] + 1]))
                    for m in range(2):
                        for k in range(2):
                            if blk < 8:
                                rhs = xT[:, (blk // 2) % 2, k, (blk % 2) * 256:(blk % 2) * 256 + 256]
                            else:
                                rhs = xeT[:, blk % 2, k * CAP:(k + 1) * CAP]
                            mm = pe.matmul(bank[0:w, m * 256:(m + 1) * 256], gu(m, k, HC[c][0], w), rhs,
                                           start=(k == 0), stop=(k == 1))
                    mm.then_inc(f_ready, 1)
                else:
                    pe.wait_ge(f_free, FU_AT[("gu", blk, 2)] + 1)
                    for t in range(2):
                        for i, (_, w) in enumerate(HC):
                            mm = pe.matmul(bank[:, t * L:(t + 1) * L], hT[0:w, blk % 2, i, t * P:(t + 1) * P],
                                           down(i, w), start=(i == 0), stop=(i == 2))
                    mm.then_inc(f_ready, 1)

            def turn_xe(e):
                n = TP_AT[("xe", e, 0)]
                tp_wait(pe, n)
                pe.wait_ge(xe_in[e % XRING], 16 * (e // XRING + 1))
                for k in range(2):
                    for t in range(2):
                        mm = pe.transpose(tp[n % 2][:, k * CAP + t * P:k * CAP + (t + 1) * P],
                                          xe[:, e % XRING, t, k * P:(k + 1) * P], ident[:, :])
                mm.then_inc(tp_ready, 1)

            pe.wait_ge(pool_consts, 1)
            turn_q(0)
            for s in range(SLOTS):
                if s < CONV:
                    convolve(s)
                g, u = tail_group(s)
                if g < NG:
                    if u == 1 and g >= 0:
                        turn_r(g)
                    if u == 3 and g >= 0:
                        turn_xT(g)
                    if u == 4 and g >= 0:
                        logits(g)
                    if u == 5 and g + 2 < NG:
                        turn_q(g + 2)
                    if u == 6 and g >= 0:
                        places(g)
                if s >= F0_SLOT:
                    feed_forward(s - F0_SLOT)
            turn_xe(0)
            for n in range(SHARED_USES, len(FU)):
                kind, blk, c = FU[n]
                feed_forward(n)
                if kind == "gu" and c == 1 and blk + 1 < 16:
                    turn_xe(blk + 1 - 8)


def lay_out(a):
    import numpy as np
    ctx = np.asarray(a["ctx_2048"])
    c = ctx.reshape(NG, GB, H, DH, BLK, P)[..., ::-1].transpose(0, 5, 2, 3, 4, 1)
    k = np.pad(np.asarray(a["L0_xattn_ssm_kernel"]), ((0, 0), (P - 1, 0)))
    f = lambda n: np.ascontiguousarray(np.asarray(a[n]))
    return {
        "x": f("x"), "ctxt": np.ascontiguousarray(c).reshape(NG, P, H * 64), "kpad": np.ascontiguousarray(k),
        "skip_d": f("L0_xattn_D"), "g_x": f("g_xattn"), "g_f": f("g_ffn"), "wg": f("L0_ffn_Wg"),
        "w1": f("L0_ffn_W1"), "w3": f("L0_ffn_W3"), "w2": f("L0_ffn_W2"),
        "sw1": f("L0_ffn_sw1"), "sw3": f("L0_ffn_sw3"), "sw2": f("L0_ffn_sw2"),
    }


def kernel(**inputs):
    import concourse.bacc as bacc
    from concourse.bass_utils import run_bass_kernel_spmd

    nc = bacc.Bacc("TRN2", target_bir_lowering=False, num_devices=1)
    arrays = lay_out(inputs)
    args = [nc.dram_tensor(name, v.shape, F32, kind="ExternalInput").ap() for name, v in arrays.items()]
    out = nc.dram_tensor("out", (B, CH, L), F32, kind="ExternalOutput").ap()
    build(nc, *args, out)
    r = run_bass_kernel_spmd(nc, [arrays], core_ids=[0])
    return r.results[0]["out"]
```

```python
from contextlib import ExitStack

import concourse.bass as bass
from concourse import mybir

F32 = mybir.dt.float32
F32R = mybir.dt.float32r
I32 = mybir.dt.int32
ALU = mybir.AluOpType
ACT = mybir.ActivationFunctionType
AX_X = mybir.AxisListType.X

P = 128
B, CH, L = 16, 128, 256
DH = 8
H = CH // DH
BLK = L // P
NG = 4
GB = B // NG
PL = BLK * GB
NPL = 36
KVH = NPL * PL
QPL = 12
CW = QPL * PL
E, HID, CAP = 8, 352, B * CH // 8
KPAD = L + P - 1
HC = (0, 128, HID - 128)
AGAIN = 2 * 128 - HC[2]
GUW, DW = 2 * 2 * HID, 3 * L
ROW = L + 2
EPS = 1e-5
UNITS = H // 2
CONV = NG * UNITS
XRING, BRING = 3, 3
F0_SLOT = 17
OUT_OF_RANGE = 4096.0
SHARED_USES = 31
SLOTS = F0_SLOT + SHARED_USES
SPLIT_SLOTS = {0: 12, 1: 18}
WIDE_USES = CONV + 2 - F0_SLOT
SGS = 3
LAG = 2
PRODS = 3
POOL_UNITS = (1, 3, 5)


def by_pool(s):
    return s % UNITS in POOL_UNITS


def pool_slots(s):
    return sum(by_pool(k) for k in range(s + 1))


def wait_products(eng, s, by_dve, by_gpsimd):
    if by_pool(s):
        eng.wait_ge(by_gpsimd, pool_slots(s))
    else:
        eng.wait_ge(by_dve, s + 1 - pool_slots(s))


STEPS = {
    "ln1_stats": 0, "ln1_scale": 1, "ln1_apply": 2, "turn_q": 4,
    "residual": 2, "ln2_stats": 3, "ln2_scale": 4, "ln2_apply": 5, "turn_xT": 6, "logits": 7,
    "exp": 7, "places": 9, "gate": 9, "scatter": 10,
}
PREPARING = ("ln1_stats", "ln1_scale", "ln1_apply", "turn_q")


def due(step, s):
    g, late = divmod(s - STEPS[step], UNITS)
    g += 1 if step in PREPARING else -1
    low = 1 if step in PREPARING else 0
    return g if late == 0 and low <= g < NG else -1


def kv_due(s):
    g, u = divmod(s, UNITS)
    return (g + 1, u // 2) if u % 2 == 0 and g + 1 < NG else (-1, 0)


def transposing_uses():
    uses = [("q", 0, 0), ("q", 0, 1)]
    for s in range(SLOTS):
        for what, step, parts in (("r", "residual", 2), ("q", "turn_q", 2), ("xT", "turn_xT", 2),
                                  ("logits", "logits", 1), ("pos", "places", 1)):
            if due(step, s) >= 0:
                uses += [(what, due(step, s), k) for k in range(parts)]
    uses += [("xe", e, 0) for e in range(E)]
    return uses


TP = transposing_uses()
TP_AT = {use: n for n, use in enumerate(TP)}
BY_ACT = {"q": True, "xT": False, "xe": False, "r": False, "logits": False, "pos": False}


def feed_forward_uses():
    uses = []
    for n in range(16):
        uses += [("gu", n, 0), ("gu", n, 1)]
        if n > 0:
            uses += [("y", n - 1, 0)]
        uses += [("gu", n, 2)]
    return uses + [("y", 15, 0)]


FU = feed_forward_uses()
FU_AT = {use: n for n, use in enumerate(FU)}
GU_SEQ = [use for use in FU if use[0] == "gu"]
GU_NUM = {use: n for n, use in enumerate(GU_SEQ)}


def rounding_due(n):
    if n == len(FU) - 1:
        return len(GU_SEQ) - 1
    return GU_NUM[FU[n]] - 1 if FU[n][0] == "gu" else -1


def weight_set(blk):
    return max(0, blk - 7)


def build(nc, x, ctxt, kpad, skip_d, g_x, g_f, wg, w1, w3, w2, sw1, sw3, sw2, out):
    xd = nc.dram_tensor("xd_scratch", (E * CAP, ROW), F32, kind="Internal").ap()
    base = nc.dram_tensor("base_scratch", (B * CH, L), F32, kind="Internal").ap()
    out_rows = out.rearrange("b c l -> (b c) l")

    with ExitStack() as ctx:
        def sb(name, shape, dt=F32):
            return ctx.enter_context(nc.sbuf_tensor(name, shape, dt))

        def sem(name):
            return ctx.enter_context(nc.semaphore(name))

        x_sb = sb("x_sb", [P, B, L])
        ct = sb("ct", [P, 2, H * CW])
        toep = sb("toep", [P, H, L])
        kv = sb("kv", [P, 2, H * KVH])
        qr = sb("qr", [P, 2, H * QPL * PL])
        prod = sb("prod", [P, PRODS, 2 * 512])
        r_sb = sb("r_sb", [P, 2, H * 64])
        zs = sb("zs", [P, 2, 2 * KVH])
        xn = sb("xn", [P, GB, L])
        xrow = sb("xrow", [P, 2, GB, ROW])
        xTh = sb("xTh", [P, 2, 2, GB * P], F32R)
        xTl = sb("xTl", [P, 2, 2, GB * P], F32R)
        wg_sb = sb("wg_sb", [P, 2, E])
        wgh = sb("wgh", [P, 2, E], F32R)
        wgl = sb("wgl", [P, 2, E], F32R)
        w_gu = sb("w_gu", [P, GUW])
        w_d = sb("w_d", [P, DW])
        wh_gu = sb("wh_gu", [P, 2, GUW], F32R)
        wl_gu = sb("wl_gu", [P, 2, GUW], F32R)
        wh_d = sb("wh_d", [P, 2, DW], F32R)
        wl_d = sb("wl_d", [P, 2, DW], F32R)
        sg = sb("sg", [P, SGS, 256])
        hTh = sb("hTh", [P, 2, 3, 256], F32R)
        hTl = sb("hTl", [P, 2, 3, 256], F32R)
        stats = sb("stats", [P, GB, 6])
        mv = sb("mv", [P, GB, 2])
        veps = sb("veps", [P, GB])
        mneg = sb("mneg", [P, GB])
        rstd = sb("rstd", [P, GB])
        nbias = sb("nbias", [P, GB])
        mhalf = sb("mhalf", [P, GB])
        ident = sb("ident", [P, P])
        anti = sb("anti", [P, P])
        tri = sb("tri", [P, P])
        ones = sb("ones", [P, P])
        d_bc = sb("d_bc", [P, H])
        gates = sb("gates", [P, 2])
        tg = sb("tg", [P, 2])
        ebase = sb("ebase", [P, GB, E])
        prio = sb("prio", [P, GB, E])
        mx = sb("mx", [P, GB])
        sh = sb("sh", [P, GB, E])
        ex = sb("ex", [P, GB, E])
        se = sb("se", [P, GB])
        gp = sb("gp", [P, GB])
        eq = sb("eq", [P, GB, E])
        ms = sb("ms", [P, GB])
        oh = sb("oh", [P, B, E])
        acc = sb("acc", [P, B + 1, E])
        t1 = sb("t1", [P, GB, E])
        t2 = sb("t2", [P, GB, E])
        t3 = sb("t3", [P, GB, E])
        slotf = sb("slotf", [P, GB])
        dest = sb("dest", [P, B], I32)
        zeros = xrow[:, 1, :, :].rearrange("p b n -> p (b n)")
        after, o = kv[:, 0, :], 0
        xe = after[:, o:o + XRING * 2 * ROW].rearrange("p (i t n) -> p i t n", i=XRING, t=2)
        o += XRING * 2 * ROW
        bg = after[:, o:o + BRING * 2 * L].rearrange("p (i t n) -> p i t n", i=BRING, t=2)
        o += BRING * 2 * L
        fin = after[:, o:o + 4 * L].rearrange("p (i t n) -> p i t n", i=2, t=2)
        w_gu2, w_d2 = kv[:, 1, 0:GUW], kv[:, 1, GUW:GUW + DW]
        tok = sb("tok", [P, E, 2], I32)
        tv = sb("tv", [P, 2])

        z = [ctx.enter_context(nc.psum_tensor(f"z{i}", [P, 2, 512], F32)) for i in range(2)]
        fb = [ctx.enter_context(nc.psum_tensor(f"fb{i}", [P, 512], F32)) for i in range(2)]
        tp = [ctx.enter_context(nc.psum_tensor(f"tp{i}", [P, 512], F32)) for i in range(2)]

        x_in = [sem(f"x_in{g}") for g in range(NG)]
        ctx_in = [sem(f"ctx_in{g}") for g in range(NG)]
        ctx_first = sem("ctx_first")
        toep_in = [sem(f"toep_in{k}") for k in range(4)]
        small_in = sem("small_in")
        weights_in = [sem(f"weights_in{w}") for w in range(2)]
        wg_high = sem("wg_high")
        wg_low = sem("wg_low")
        w_high = sem("w_high")
        w_low_dve = sem("w_low_dve")
        w_low_pool = sem("w_low_pool")
        xd_zeroed = sem("xd_zeroed")
        pool_consts = sem("pool_consts")
        dve_consts = sem("dve_consts")
        tanh_done = sem("tanh_done")
        diag_added = sem("diag_added")
        kv_pool = sem("kv_pool")
        kv_dve = sem("kv_dve")
        kv_square = sem("kv_square")
        stats_done = sem("stats_done")
        rstd_done = sem("rstd_done")
        xn_done = sem("xn_done")
        xrow_done = sem("xrow_done")
        q_done = sem("q_done")
        z_ready = sem("z_ready")
        prods = sem("prods")
        zs_done = sem("zs_done")
        prods_pool = sem("prods_pool")
        reduced = sem("reduced")
        tp_ready = sem("tp_ready")
        tp_free_act = sem("tp_free_act")
        tp_free_dve = sem("tp_free_dve")
        f_ready = sem("f_ready")
        silu_done = sem("silu_done")
        x_high = sem("x_high")
        h_high = sem("h_high")
        h_low = sem("h_low")
        f_free = sem("f_free")
        shifted = sem("shifted")
        exp_done = sem("exp_done")
        onehot = sem("onehot")
        gate_done = sem("gate_done")
        dest_done = sem("dest_done")
        link = sem("link")
        plink = sem("plink")
        scattered = [sem(f"scattered{i}") for i in range(2)]
        numbered = sem("numbered")
        base_stored = sem("base_stored")
        xe_in = [sem(f"xe_in{i}") for i in range(XRING)]
        tok_done = sem("tok_done")
        gathered = [sem(f"gathered{i}") for i in range(BRING)]
        stored = [sem(f"stored{i}") for i in range(2)]

        def view(t, off, dims, parts=P):
            a = t[:]
            row = a.ap[0][0]
            return bass.AP(a.tensor, a.offset + off, [[row, parts], *dims])

        def tp_wait(eng, n):
            if n >= 2:
                by_act = BY_ACT[TP[n - 2][0]]
                count = sum(BY_ACT[TP[k][0]] == by_act for k in range(n - 1))
                eng.wait_ge(tp_free_act if by_act else tp_free_dve, count)

        def f_bank(n):
            if n < WIDE_USES:
                return fb[n % 2][:, :], n - 2
            m = n - WIDE_USES + WIDE_USES % 2
            k = m % 6
            bank = fb[k][:, :] if k < 2 else z[(k - 2) // 2][:, k % 2, :]
            if m < 2:
                return bank, n - 2
            return bank, (n - 6 if m >= 6 else None)

        def plain(ap):
            return ap.bitcast(F32)

        def as_loaded(w):
            if w >= 2 and w % 2 == 0:
                return w_gu2, w_d2, weights_in[1], 64 * (w // 2)
            return w_gu[:, :], w_d[:, :], weights_in[0], 64 * ((w + 1) // 2 + 1)

        def turned(n):
            return sum(use[0] in ("xT", "xe") for use in TP[:n + 1])

        def wait_high(eng, w, part):
            eng.wait_ge(w_high, 2 * w + part + 1)

        def weights_split(eng, w):
            eng.wait_ge(w_low_dve, 2 * w + 2)
            eng.wait_ge(w_low_pool, w + 1)

        norms = [("ln1", 0)]
        for s in range(SLOTS):
            norms += [(what, due(what + "_stats", s)) for what in ("ln1", "ln2") if due(what + "_stats", s) >= 0]
        NORM_AT = {what: n for n, what in enumerate(norms)}

        def norm_read(eng, n):
            what, g = norms[n]
            eng.wait_ge(xn_done if what == "ln1" else xrow_done, g + 1)

        def load_rows(sp, e):
            if e == 0:
                for i in range(2):
                    sp.wait_ge(scattered[i], 16 * B // 2)
            if e >= XRING:
                sp.wait_ge(tp_ready, TP_AT[("xe", e - XRING, 0)] + 1)
                sp.wait_ge(tok_done, e - XRING + 1)
                sp.wait_ge(f_free, FU_AT[("y", 8 + e - XRING, 0)] + 1)
            sp.dma_start(xe[:, e % XRING, :, :],
                         xd[e * CAP:(e + 1) * CAP, :].rearrange("(t p) n -> p t n", p=P)).then_inc(xe_in[e % XRING], 16)

        def kv_planes(g, c, o, a, dims_kv, dims_ct):
            return (view(kv, (g % 2) * H * KVH + 4 * c * KVH + o, [[KVH, 4], *dims_kv]),
                    view(ct, (g % 2) * H * CW + 4 * c * CW + a, [[CW, 4], *dims_ct]))

        def kv_products(eng, g, c, first, done):
            n = 4 - first
            dst, left = kv_planes(g, c, 64 * first, 0, [[64, n], [1, 64]], [[0, n], [1, 64]])
            _, right = kv_planes(g, c, 0, PL * first, [], [[PL, n], [1, 64]])
            eng.tensor_tensor(dst, left, right, ALU.mult)
            dst, left = kv_planes(g, c, 256, 0, [[1, 32]], [[1, 32]])
            _, right = kv_planes(g, c, 0, 32, [], [[1, 32]])
            eng.tensor_tensor(dst, left, right, ALU.mult).then_inc(done, 1)

        def kv_place_free(eng, g):
            eng.wait_ge(ctx_in[g], 16)
            if g >= 2:
                eng.wait_ge(z_ready, UNITS * (g - 1))

        def multiply(eng, s, src, zc, stride):
            g, u = divmod(s, UNITS)
            q0 = (g % 2) * H * CW + 2 * u * CW
            p0 = (s % PRODS) * 1024

            def mul(o, zo, qo, od, zd, qd):
                return eng.tensor_tensor(view(prod, p0 + o, [[512, 2], *od]), view(src, zc + zo, [[stride, 2], *zd]),
                                         view(qr, q0 + qo, [[CW, 2], *qd]), ALU.mult)
            mul(0, 0, 0, [[64, 4], [1, 64]], [[64, 4], [1, 64]], [[PL, 4], [1, 64]])
            mul(256, 256, 32, [[32, 2], [1, 32]], [[0, 2], [1, 32]], [[32, 2], [1, 32]])
            mul(320 + 8, 64, 0, [[72, 2], [1, 64]], [[64, 2], [1, 64]], [[0, 2], [1, 64]])
            mul(448 + 24, 192, 0, [[1, 40]], [[1, 40]], [[1, 40]])
            return mul(320, 192 + 40, 40, [[72, 3], [1, 8]], [[8, 3], [1, 8]], [[8, 3], [1, 8]])

        block = ctx.enter_context(nc.Block())

        @block.sync
        def _(sp):
            def load_ctx(g):
                if g >= 2:
                    sp.wait_ge(kv_pool, 4 * (g - 2) + 3)
                    sp.wait_ge(kv_square, 4 * (g - 2) + 3)
                    if g == 2:
                        sp.wait_ge(kv_dve, 1)
                sp.dma_start(ct[:, g % 2, :], ctxt[g]).then_inc(ctx_in[g], 16)

            def load_x(g):
                sp.dma_start(x_sb[:, GB * g:GB * (g + 1), :],
                             x[GB * g:GB * (g + 1)].rearrange("b c l -> c b l")).then_inc(x_in[g], 16)

            def load_toeplitz(k):
                src = bass.AP(kpad.tensor, kpad.offset + 4 * k * KPAD, [[1, P], [KPAD, 4], [1, L]])
                sp.dma_start(toep[:, 4 * k:4 * k + 4, :], src).then_inc(toep_in[k], 16)

            def load_weights(w):
                if w == 2:
                    sp.wait_ge(z_ready, CONV)
                elif w >= 1:
                    weights_split(sp, max(0, w - 2))
                a1, a3, a2 = (sw1, sw3, sw2) if w == 0 else (w1[w - 1], w3[w - 1], w2[w - 1])
                gu, down, done, _ = as_loaded(w)
                for m, a in ((0, a1), (1, a3)):
                    sp.dma_start(gu[:, m * 2 * HID:(m + 1) * 2 * HID].rearrange("p (k n) -> p k n", k=2),
                                 a.rearrange("(k p) n -> p k n", p=P)).then_inc(done, 16)
                sp.dma_start(down[:, 0:2 * L].rearrange("p (k n) -> p k n", k=2),
                             a2[0:256, :].rearrange("(k p) n -> p k n", p=P)).then_inc(done, 16)
                sp.dma_start(down[AGAIN:P, 2 * L:3 * L], a2[256:HID, :]).then_inc(done, 16)

            sp.dma_start(ct[:, 0, 0:4 * CW], ctxt[0, :, 0:4 * CW]).then_inc(ctx_first, 16)
            load_toeplitz(0)
            load_x(0)
            sp.dma_start(d_bc[:, :], bass.AP(skip_d.tensor, skip_d.offset, [[0, P], [1, H]])).then_inc(small_in, 16)
            sp.dma_start(ct[:, 0, 4 * CW:], ctxt[0, :, 4 * CW:]).then_inc(ctx_in[0], 16)
            sp.dma_start(gates[:, 0:1], bass.AP(g_x.tensor, g_x.offset, [[0, P], [1, 1]])).then_inc(small_in, 16)
            sp.dma_start(gates[:, 1:2], bass.AP(g_f.tensor, g_f.offset, [[0, P], [1, 1]])).then_inc(small_in, 16)
            sp.dma_start(wg_sb[:, :, :], wg.rearrange("(k p) e -> p k e", p=P)).then_inc(small_in, 16)
            for k in range(1, 4):
                load_toeplitz(k)
            load_ctx(1)
            load_x(1)
            load_weights(0)
            load_x(2)
            load_x(3)
            load_ctx(2)
            sp.wait_ge(dve_consts, 5)
            xd_flat = xd.rearrange("(p q r) n -> q p (r n)", p=P, q=4)
            for k in range(4):
                sp.dma_start(xd_flat[k], zeros).then_inc(xd_zeroed, 16)
            load_ctx(3)
            load_weights(1)
            load_weights(3)
            for n in range(8):
                sp.wait_ge(f_free, FU_AT[("y", n, 0)] + 1)
                for dst in (out, base.rearrange("(b c) l -> b c l", c=CH)):
                    sp.dma_start(dst[2 * n:2 * n + 2].rearrange("b c l -> c b l"),
                                 x_sb[:, 2 * n:2 * n + 2, :]).then_inc(base_stored, 16)
                if n == 3:
                    load_weights(2)
                if n == 6:
                    for e in range(2):
                        load_rows(sp, e)
            for e in range(2, E):
                load_rows(sp, e)
                if e + 2 <= E:
                    load_weights(e + 2)
            for i in range(2):
                sp.wait_ge(stored[i], 16 * 2 * (E // 2))

        @block.gpsimd
        def _(pool):
            linked = [0]

            def chain(ins):
                linked[0] += 1
                ins.then_inc(plink, 1)
                pool.wait_ge(plink, linked[0])

            def scale_and_bias(n):
                pool.wait_ge(stats_done, n + 1)
                if n >= 1:
                    norm_read(pool, n - 1)
                chain(pool.tensor_tensor(rstd[:, :], veps[:, :], mhalf[:, :], ALU.pow))
                pool.tensor_tensor(nbias[:, :], mneg[:, :], rstd[:, :], ALU.mult).then_inc(rstd_done, 1)

            chain(pool.memset(ident[:, :], 0.0))
            pool.affine_select(out=ident[:, :], in_=ident[:, :], compare_op=ALU.not_equal, fill=1.0, base=0,
                               pattern=[[-1, P]], channel_multiplier=1).then_inc(pool_consts, 1)
            chain(pool.memset(anti[:, :], 0.0))
            pool.affine_select(out=anti[:, :], in_=anti[:, :], compare_op=ALU.not_equal, fill=1.0, base=1 - P,
                               pattern=[[1, P]], channel_multiplier=1).then_inc(pool_consts, 1)
            pool.wait_ge(dve_consts, 5)
            kv_place_free(pool, 0)
            kv_products(pool, 0, 1, 1, kv_pool)
            scale_and_bias(0)
            for c in range(2, 4):
                kv_products(pool, 0, c, 1, kv_pool)
            pool.affine_select(out=tri[:, :], in_=ones[:, :], compare_op=ALU.is_ge, fill=0.0, base=-1,
                               pattern=[[1, P]], channel_multiplier=-1).then_inc(pool_consts, 1)
            pool.iota(ebase[:, :, :], pattern=[[0, GB], [CAP, E]], base=0, channel_multiplier=0,
                      allow_small_or_imprecise_dtypes=True).then_inc(pool_consts, 1)
            pool.iota(prio[:, :, :], pattern=[[0, GB], [-1, E]], base=E, channel_multiplier=0,
                      allow_small_or_imprecise_dtypes=True).then_inc(pool_consts, 1)
            def split_up(w):
                wait_high(pool, w, 0)
                up = slice(2 * HID, 4 * HID)
                pool.tensor_tensor(wl_gu[:, w % 2, up], as_loaded(w)[0][:, up], plain(wh_gu[:, w % 2, up]),
                                   ALU.subtract).then_inc(w_low_pool, 1)

            for s in range(SLOTS):
                for what in ("ln1", "ln2"):
                    if due(what + "_scale", s) >= 0:
                        scale_and_bias(NORM_AT[(what, due(what + "_scale", s))])
                if s < CONV and by_pool(s):
                    k = pool_slots(s)
                    pool.wait_ge(zs_done, k)
                    pool.wait_ge(q_done, s // UNITS + 1)
                    if s >= PRODS:
                        pool.wait_ge(reduced, s - PRODS + 1)
                    multiply(pool, s, zs, ((k - 1) % 2) * 2 * KVH, KVH).then_inc(prods_pool, 1)
                g, c = kv_due(s)
                if g >= 0:
                    kv_place_free(pool, g)
                    kv_products(pool, g, c, 1, kv_pool)
                if s == CONV:
                    pool.wait_ge(z_ready, CONV)
                    pool.memset(bg[:, :, :, :], 0.0).then_inc(pool_consts, 1)
                    pool.memset(w_d2[0:AGAIN, 2 * L:3 * L], 0.0).then_inc(pool_consts, 1)
                g = due("scatter", s)
                if g >= 0:
                    if g == 0:
                        pool.wait_ge(xd_zeroed, 16 * 4)
                    if g >= 2:
                        pool.wait_ge(scattered[g % 2], 16 * GB)
                    pool.iota(xrow[:, g % 2, :, L + 1:L + 2], pattern=[[P, GB], [1, 1]], base=1 + g * GB * P,
                              channel_multiplier=1, allow_small_or_imprecise_dtypes=True).then_inc(numbered, 1)
                    pool.wait_ge(numbered, g + 1)
                    pool.wait_ge(dest_done, g + 1)
                    pool.wait_ge(gate_done, g + 1)
                    for b in range(GB * g, GB * (g + 1)):
                        pool.indirect_dma_start(
                            out=xd, out_offset=bass.IndirectOffsetOnAxis(ap=dest[:, b:b + 1], axis=0),
                            in_=xrow[:, g % 2, b % GB, :], in_offset=None, bounds_check=E * CAP - 1,
                            oob_is_err=False).then_inc(scattered[g % 2], 16)
                for w in SPLIT_SLOTS:
                    if s == SPLIT_SLOTS[w]:
                        split_up(w)

            def gather(e):
                pool.wait_ge(tok_done, e + 1)
                if e == 0:
                    pool.wait_ge(base_stored, 16 * 16)
                    pool.wait_ge(pool_consts, 7)
                if e >= BRING:
                    pool.wait_ge(f_free, FU_AT[("y", 8 + e - BRING, 0)] + 1)
                for t in range(2):
                    pool.indirect_dma_start(
                        out=bg[:, e % BRING, t, :], out_offset=None, in_=base,
                        in_offset=bass.IndirectOffsetOnAxis(ap=tok[:, e, t:t + 1], axis=0),
                        bounds_check=B * CH - 1, oob_is_err=False).then_inc(gathered[e % BRING], 16)

            split_up(2)
            gather(0)
            for e in range(E):
                if e + 1 < E:
                    gather(e + 1)
                if e + 3 <= E:
                    split_up(e + 3)
                pool.wait_ge(f_free, FU_AT[("y", 8 + e, 0)] + 1)
                for t in range(2):
                    pool.indirect_dma_start(
                        out=out_rows, out_offset=bass.IndirectOffsetOnAxis(ap=tok[:, e, t:t + 1], axis=0),
                        in_=fin[:, e % 2, t, :], in_offset=None, bounds_check=B * CH - 1,
                        oob_is_err=False).then_inc(stored[e % 2], 16)

        @block.scalar
        def _(act):
            def normalise(n, dst, free):
                what, g = norms[n]
                act.wait_ge(rstd_done, n + 1)
                free()
                for b in range(GB):
                    last = act.activation(dst(b), x_sb[:, GB * g + b, :], ACT.Identity,
                                          bias=nbias[:, b:b + 1], scale=rstd[:, b:b + 1])
                last.then_inc(xn_done if what == "ln1" else xrow_done, 1)

            def norm1(g):
                def free():
                    if g >= 1:
                        act.wait_ge(tp_ready, TP_AT[("q", g - 1, 1)] + 1)
                normalise(NORM_AT[("ln1", g)], lambda b: xn[:, b, :], free)

            def norm2(g):
                def free():
                    if g == 1:
                        act.wait_ge(xd_zeroed, 16 * 4)
                    if g >= 2:
                        act.wait_ge(scattered[g % 2], 16 * GB)
                normalise(NORM_AT[("ln2", g)], lambda b: xrow[:, g % 2, b, 0:L], free)

            def squares(g, c):
                kv_place_free(act, g)
                dst, src = kv_planes(g, c, 0, 0, [[1, 64]], [[1, 64]])
                act.activation(dst, src, ACT.Square).then_inc(kv_square, 1)

            def z_copy(s):
                k = pool_slots(s)
                act.wait_ge(z_ready, s + 1)
                if k > 2:
                    act.wait_ge(prods_pool, k - 2)
                act.activation(view(zs, ((k - 1) % 2) * 2 * KVH, [[KVH, 2], [1, KVH]]),
                               z[s % 2][:, :, 0:KVH], ACT.Copy).then_inc(zs_done, 1)

            def q_copy(g):
                o = (g % 2) * H * QPL * PL
                if g >= 2:
                    act.wait_ge(prods_pool, pool_slots(UNITS * (g - 1) - 1))
                    act.wait_ge(prods, UNITS * (g - 1) - pool_slots(UNITS * (g - 1) - 1))
                for k in range(BLK):
                    n = TP_AT[("q", g, k)]
                    act.wait_ge(tp_ready, n + 1)
                    act.activation(view(qr, o + GB * k, [[QPL * PL, H], [PL, DH], [1, GB]]),
                                   view(tp[n % 2], 0, [[DH, H], [1, DH], [P, GB]]),
                                   ACT.Copy).then_inc(tp_free_act, 1)
                act.wait_ge(tp_free_act, sum(BY_ACT[k[0]] for k in TP[:TP_AT[("q", g, 1)] + 1]))
                act.activation(view(qr, o + DH * PL, [[QPL * PL, H], [1, 4 * PL]]),
                               view(qr, o, [[QPL * PL, H], [1, 4 * PL]]), ACT.Copy).then_inc(q_done, 1)

            def xT_high(g):
                if g >= 2:
                    act.wait_ge(f_ready, FU_AT[("gu", 2 * (g - 2) + 1, 2)] + 1)
                for k in range(2):
                    n = TP_AT[("xT", g, k)]
                    act.wait_ge(tp_ready, n + 1)
                    act.activation(xTh[:, g % 2, k, :], tp[n % 2][:, :], ACT.Copy).then_inc(x_high, 1)

            def exponentials(g):
                act.wait_ge(shifted, g + 1)
                if g >= 1:
                    act.wait_ge(gate_done, g)
                act.activation(ex[:, :, :], sh[:, :, :], ACT.Exp).then_inc(exp_done, 1)

            def silu(n):
                kind, blk, c = FU[n]
                if kind != "gu":
                    return
                k = GU_NUM[FU[n]]
                act.wait_ge(f_ready, n + 1)
                if k >= SGS:
                    act.wait_ge(h_low, k - SGS + 1)
                bank, _ = f_bank(n)
                act.activation(sg[:, k % SGS, :], bank[:, 0:256], ACT.Silu).then_inc(silu_done, 1)

            def hidden_high(n):
                k = rounding_due(n)
                if k < 0:
                    return
                _, blk, c = GU_SEQ[k]
                act.wait_ge(f_free, FU_AT[GU_SEQ[k]] + 1)
                if blk >= 2:
                    act.wait_ge(f_ready, FU_AT[("y", blk - 2, 0)] + 1)
                act.activation(hTh[:, blk % 2, c, :], sg[:, k % SGS, :], ACT.Copy).then_inc(h_high, 1)

            def xe_high(e):
                n = TP_AT[("xe", e, 0)]
                act.wait_ge(tp_ready, n + 1)
                act.wait_ge(f_ready, FU_AT[("gu", (5, 7)[e] if e < 2 else 8 + e - 2, 2)] + 1)
                act.activation(xTh[:, e % 2, :, 0:CAP], tp[n % 2][:, :].rearrange("p (k n) -> p k n", k=2),
                               ACT.Copy).then_inc(x_high, 1)

            def weights_high(w, part):
                i = w % 2
                gu, down, done, count = as_loaded(w)
                if part == 0:
                    act.wait_ge(done, count)
                elif w == 2:
                    act.wait_ge(pool_consts, 7)
                if w >= 2:
                    before = w + 7 - 2
                    act.wait_ge(f_ready, FU_AT[("gu", before, 2) if part == 0 else ("y", before, 0)] + 1)
                src, dst = ((gu, wh_gu), (down, wh_d))[part]
                act.activation(dst[:, i, :], src, ACT.Copy).then_inc(w_high, 1)

            act.wait_ge(small_in, 16 * 4)
            act.activation(tg[:, :], gates[:, :], ACT.Tanh).then_inc(tanh_done, 1)
            act.activation(wgh[:, :, :], wg_sb[:, :, :], ACT.Copy).then_inc(wg_high, 1)
            norm1(0)
            for c in range(1, 4):
                squares(0, c)
            q_copy(0)
            for s in range(SLOTS):
                if s < CONV and by_pool(s):
                    z_copy(s)
                if s >= F0_SLOT:
                    silu(s - F0_SLOT)
                    hidden_high(s - F0_SLOT)
                if kv_due(s)[0] >= 0:
                    squares(*kv_due(s))
                if due("ln1_apply", s) >= 0:
                    norm1(due("ln1_apply", s))
                if due("turn_q", s) >= 0:
                    q_copy(due("turn_q", s))
                if due("ln2_apply", s) >= 0:
                    norm2(due("ln2_apply", s))
                if due("turn_xT", s) >= 0:
                    xT_high(due("turn_xT", s))
                if due("exp", s) >= 0:
                    exponentials(due("exp", s))
                for w in SPLIT_SLOTS:
                    if s == SPLIT_SLOTS[w]:
                        weights_high(w, 0)
                        weights_high(w, 1)
            xe_high(0)
            for n in range(SHARED_USES, len(FU)):
                kind, blk, c = FU[n]
                silu(n)
                hidden_high(n)
                if kind == "gu" and blk + 1 < 16:
                    if c == 0:
                        weights_high(weight_set(blk) + 1, 0)
                    elif c == 1:
                        xe_high(blk + 1 - 8)
                    else:
                        weights_high(weight_set(blk) + 1, 1)

        @block.vector
        def _(dve):
            linked = [0]

            def chain(ins):
                linked[0] += 1
                ins.then_inc(link, 1)
                dve.wait_ge(link, linked[0])

            def norm_stats(n):
                what, g = norms[n]
                if n >= 1:
                    dve.wait_ge(rstd_done, n)
                for b in range(GB):
                    ins = dve.bn_stats(stats[:, b, :], x_sb[:, GB * g + b, :])
                chain(ins)
                for b in range(GB):
                    ins = dve.bn_aggr(mv[:, b, :], stats[:, b, :])
                chain(ins)
                dve.tensor_scalar(veps[:, :], mv[:, :, 1], EPS, None, ALU.add)
                dve.tensor_scalar(mneg[:, :], mv[:, :, 0], -1.0, None, ALU.mult).then_inc(stats_done, 1)

            def products(s):
                dve.wait_ge(z_ready, s + 1)
                dve.wait_ge(q_done, s // UNITS + 1)
                if s >= PRODS:
                    dve.wait_ge(reduced, s - PRODS + 1)
                multiply(dve, s, z[s % 2], 0, 512).then_inc(prods, 1)

            def add_terms(s):
                g, u = divmod(s, UNITS)
                wait_products(dve, s, prods, prods_pool)
                if g >= 2 and u == 0:
                    dve.wait_ge(tp_ready, TP_AT[("r", g - 2, 1)] + 1)
                o = (g % 2) * H * 64 + 2 * u * 64
                dve.tensor_reduce(view(r_sb, o, [[64, 2], [1, 64]]),
                                  view(prod, (s % PRODS) * 1024, [[512, 2], [1, 64], [64, 8]]),
                                  AX_X, ALU.add).then_inc(reduced, 1)

            def first_residual(g):
                for k in range(2):
                    n = TP_AT[("r", g, k)]
                    dve.wait_ge(tp_ready, n + 1)
                    if g == 0 and k == 0:
                        dve.wait_ge(tanh_done, 1)
                    xb = x_sb[:, GB * g + 2 * k:GB * g + 2 * k + 2, :].rearrange("p b l -> p (b l)")
                    ins = dve.scalar_tensor_tensor(out=xb, in0=tp[n % 2][:, :], scalar=tg[:, 0:1], in1=xb,
                                                   op0=ALU.mult, op1=ALU.add)
                    ins.then_inc(tp_free_dve, 1)
                dve.wait_ge(tp_free_dve, sum(not BY_ACT[k[0]] for k in TP[:n + 1]))

            def bcast(t):
                return view(t, 0, [[1, GB], [0, E]])

            def choose(g):
                n = TP_AT[("logits", g, 0)]
                lg = view(tp[n % 2], 0, [[E, GB], [1, E]])
                dve.wait_ge(tp_ready, n + 1)
                if g == 0:
                    dve.wait_ge(pool_consts, 5)
                if g >= 1:
                    dve.wait_ge(exp_done, g)
                chain(dve.tensor_reduce(mx[:, :], lg, AX_X, ALU.max))
                dve.tensor_tensor(sh[:, :, :], lg, bcast(mx), ALU.subtract).then_inc(shifted, 1)
                dve.wait_ge(shifted, g + 1)
                dve.tensor_scalar(eq[:, :, :], sh[:, :, :], 0.0, None, ALU.is_equal).then_inc(tp_free_dve, 1)
                dve.wait_ge(tp_free_dve, sum(not BY_ACT[k[0]] for k in TP[:n + 1]))
                chain(dve.tensor_tensor(t1[:, :, :], eq[:, :, :], prio[:, :, :], ALU.mult))
                chain(dve.tensor_reduce(ms[:, :], t1[:, :, :], AX_X, ALU.max))
                o = oh[:, GB * g:GB * (g + 1), :]
                chain(dve.tensor_tensor(o, t1[:, :, :], bcast(ms), ALU.is_equal))
                for b in range(GB * g, GB * (g + 1)):
                    ins = dve.tensor_tensor(acc[:, b + 1, :], acc[:, b, :], oh[:, b, :], ALU.add)
                    if b < GB * (g + 1) - 1:
                        chain(ins)
                ins.then_inc(onehot, 1)
                dve.wait_ge(onehot, g + 1)

            def gate(g):
                dve.wait_ge(exp_done, g + 1)
                chain(dve.tensor_reduce(se[:, :], ex[:, :, :], AX_X, ALU.add))
                chain(dve.reciprocal(gp[:, :], se[:, :]))
                if g == 1:
                    dve.wait_ge(xd_zeroed, 16 * 4)
                if g >= 2:
                    dve.wait_ge(scattered[g % 2], 16 * GB)
                dve.tensor_scalar(xrow[:, g % 2, :, L], gp[:, :], tg[:, 1:2], None,
                                  ALU.mult).then_inc(gate_done, 1)

            def slot_of_token(g):
                n = TP_AT[("pos", g, 0)]
                pos = view(tp[n % 2], 0, [[E, GB], [1, E]])
                dve.wait_ge(tp_ready, n + 1)
                chain(dve.tensor_scalar(t1[:, :, :], pos, float(CAP), OUT_OF_RANGE, ALU.is_ge, ALU.mult))
                ins = dve.tensor_tensor(t2[:, :, :], pos, t1[:, :, :], ALU.add)
                ins.then_inc(tp_free_dve, 1)
                dve.wait_ge(tp_free_dve, sum(not BY_ACT[k[0]] for k in TP[:n + 1]))
                chain(dve.tensor_tensor(t3[:, :, :], t2[:, :, :], ebase[:, :, :], ALU.add))
                chain(dve.tensor_tensor(t2[:, :, :], t3[:, :, :], oh[:, GB * g:GB * (g + 1), :], ALU.mult))
                chain(dve.tensor_reduce(slotf[:, :], t2[:, :, :], AX_X, ALU.add))
                dve.tensor_copy(dest[:, GB * g:GB * (g + 1)], slotf[:, :]).then_inc(dest_done, 1)

            def feed_forward(n):
                kind, blk, c = FU[n]
                bank, _ = f_bank(n)
                if kind == "gu":
                    k = GU_NUM[FU[n]]
                    dve.wait_ge(silu_done, k + 1)
                    dve.tensor_tensor(sg[:, k % SGS, :], bank[:, 256:512], sg[:, k % SGS, :],
                                      ALU.mult).then_inc(f_free, 1)
                elif blk < 8:
                    dve.wait_ge(f_ready, n + 1)
                    xb = x_sb[:, 2 * blk:2 * blk + 2, :].rearrange("p b l -> p (b l)")
                    dve.scalar_tensor_tensor(out=xb, in0=bank, scalar=tg[:, 1:2], in1=xb,
                                             op0=ALU.mult, op1=ALU.add).then_inc(f_free, 1)
                else:
                    e = blk - 8
                    dve.wait_ge(f_ready, n + 1)
                    dve.wait_ge(gathered[e % BRING], 32 * (e // BRING + 1))
                    if e >= 2:
                        dve.wait_ge(stored[e % 2], 32 * (e // 2))
                    for t in range(2):
                        ins = dve.scalar_tensor_tensor(
                            out=fin[:, e % 2, t, :], in0=bank[:, t * L:(t + 1) * L],
                            scalar=xe[:, e % XRING, t, L:L + 1], in1=bg[:, e % BRING, t, :],
                            op0=ALU.mult, op1=ALU.add)
                    ins.then_inc(f_free, 1)

            def turned_low(what, g, k, place):
                n = TP_AT[(what, g, k)]
                dve.wait_ge(x_high, turned(n))
                if what == "xT":
                    src, high, low = tp[n % 2][:, :], xTh[:, place, k, :], xTl[:, place, k, :]
                else:
                    src = tp[n % 2][:, :].rearrange("p (k n) -> p k n", k=2)
                    high, low = xTh[:, place, :, 0:CAP], xTl[:, place, :, 0:CAP]
                dve.tensor_tensor(low, src, plain(high), ALU.subtract).then_inc(tp_free_dve, 1)

            def hidden_low(n):
                k = rounding_due(n)
                if k < 0:
                    return
                _, blk, c = GU_SEQ[k]
                dve.wait_ge(h_high, k + 1)
                if blk >= 2:
                    dve.wait_ge(f_ready, FU_AT[("y", blk - 2, 0)] + 1)
                dve.tensor_tensor(hTl[:, blk % 2, c, :], sg[:, k % SGS, :], plain(hTh[:, blk % 2, c, :]),
                                  ALU.subtract).then_inc(h_low, 1)

            def weights_low(w, part):
                wait_high(dve, w, part)
                i = w % 2
                gu, down, _, _ = as_loaded(w)
                raw, high, low, cols = ((gu, wh_gu, wl_gu, slice(0, 2 * HID)), (down, wh_d, wl_d, slice(0, DW)))[part]
                dve.tensor_tensor(low[:, i, cols], raw[:, cols], plain(high[:, i, cols]),
                                  ALU.subtract).then_inc(w_low_dve, 1)

            def tokens_of_slots(e):
                dve.wait_ge(xe_in[e % XRING], 16 * (e // XRING + 1))
                v = xe[:, e % XRING, :, L + 1]
                chain(dve.tensor_scalar(tv[:, :], v, 0.0, OUT_OF_RANGE, ALU.is_equal, ALU.mult))
                ins = dve.scalar_tensor_tensor(out=tok[:, e, :], in0=tv[:, :], scalar=-1.0, in1=v,
                                               op0=ALU.add, op1=ALU.add)
                ins.then_inc(tok_done, 1)
                dve.wait_ge(tok_done, e + 1)

            dve.memset(mhalf[:, :], -0.5).then_inc(dve_consts, 1)
            dve.memset(ones[:, :], 1.0).then_inc(dve_consts, 1)
            dve.memset(zeros, 0.0).then_inc(dve_consts, 1)
            dve.memset(acc[:, 0, :], 0.0).then_inc(dve_consts, 1)
            dve.memset(w_d[0:AGAIN, 2 * L:3 * L], 0.0).then_inc(dve_consts, 1)
            dve.wait_ge(dve_consts, 5)

            def add_skip(k):
                dve.wait_ge(toep_in[k], 16)
                for h in range(4 * k, 4 * k + 4):
                    dve.scalar_tensor_tensor(out=toep[:, h, 0:P], in0=anti[:, :], scalar=d_bc[:, h:h + 1],
                                             in1=toep[:, h, 0:P], op0=ALU.mult, op1=ALU.add).then_inc(diag_added, 1)

            dve.wait_ge(ctx_first, 16)
            kv_products(dve, 0, 0, 0, kv_dve)
            dve.wait_ge(x_in[0], 16)
            norm_stats(0)
            dve.wait_ge(small_in, 16 * 4)
            dve.wait_ge(pool_consts, 2)
            for k in range(4):
                add_skip(k)
            dve.wait_ge(wg_high, 1)
            dve.tensor_tensor(wgl[:, :, :], wg_sb[:, :, :], plain(wgh[:, :, :]), ALU.subtract).then_inc(wg_low, 1)
            for s in range(SLOTS):
                if s < CONV and not by_pool(s):
                    products(s)
                if LAG <= s < CONV + LAG:
                    add_terms(s - LAG)
                if s >= F0_SLOT:
                    feed_forward(s - F0_SLOT)
                    hidden_low(s - F0_SLOT)
                if due("residual", s) >= 0:
                    first_residual(due("residual", s))
                if due("ln1_stats", s) >= 0:
                    dve.wait_ge(x_in[due("ln1_stats", s)], 16)
                    norm_stats(NORM_AT[("ln1", due("ln1_stats", s))])
                if due("ln2_stats", s) >= 0:
                    norm_stats(NORM_AT[("ln2", due("ln2_stats", s))])
                if due("logits", s) >= 0:
                    choose(due("logits", s))
                if due("places", s) >= 0:
                    slot_of_token(due("places", s))
                if due("gate", s) >= 0:
                    gate(due("gate", s))
                if due("turn_xT", s) >= 0:
                    for k in range(2):
                        turned_low("xT", due("turn_xT", s), k, due("turn_xT", s) % 2)
                for w in SPLIT_SLOTS:
                    if s == SPLIT_SLOTS[w]:
                        weights_low(w, 0)
                        weights_low(w, 1)
            turned_low("xe", 0, 0, 0)
            tokens_of_slots(0)
            for n in range(SHARED_USES, len(FU)):
                kind, blk, c = FU[n]
                if n == len(FU) - 1:
                    hidden_low(n)
                feed_forward(n)
                if n < len(FU) - 1:
                    hidden_low(n)
                if kind == "gu" and blk + 1 < 16:
                    if c == 0:
                        weights_low(weight_set(blk) + 1, 0)
                    elif c == 1:
                        turned_low("xe", blk + 1 - 8, 0, (blk + 1) % 2)
                        tokens_of_slots(blk + 1 - 8)
                    else:
                        weights_low(weight_set(blk) + 1, 1)

        @block.tensor
        def _(pe):
            def convolve(s):
                g, u = divmod(s, UNITS)
                c = u // 2
                if g == 0 and c == 0:
                    pe.wait_ge(kv_dve, 1)
                else:
                    pe.wait_ge(kv_pool, 4 * g + c)
                    pe.wait_ge(kv_square, 4 * g + c)
                if g == 0:
                    pe.wait_ge(diag_added, 2 * u + 2)
                if s >= 2:
                    wait_products(pe, s - 2, prods, zs_done)
                for k in range(2):
                    h = 2 * u + k
                    o = (g % 2) * H * KVH + h * KVH
                    pe.matmul(view(z[s % 2], k * 512 + GB, [[PL, NPL], [1, GB]]), toep[:, h, P:2 * P],
                              view(kv, o, [[PL, NPL], [1, GB]]), start=True, stop=False,
                              skip_group_check=True)
                    mm = pe.matmul(z[s % 2][:, k, 0:KVH], toep[:, h, 0:P], view(kv, o, [[1, KVH]]),
                                   start=False, stop=True, skip_group_check=True)
                mm.then_inc(z_ready, 1)

            def turn_q(g):
                pe.wait_ge(xn_done, g + 1)
                for k in range(BLK):
                    n = TP_AT[("q", g, k)]
                    tp_wait(pe, n)
                    for b in range(GB):
                        mm = pe.transpose(tp[n % 2][:, b * P:(b + 1) * P], xn[:, b, k * P:(k + 1) * P], ident[:, :])
                    mm.then_inc(tp_ready, 1)

            def turn_r(g):
                pe.wait_ge(reduced, UNITS * (g + 1))
                for k in range(2):
                    n = TP_AT[("r", g, k)]
                    tp_wait(pe, n)
                    for j in range(2 * BLK):
                        b, blk = 2 * k + j // BLK, j % BLK
                        src = view(r_sb, (g % 2) * H * 64 + blk * GB + b, [[PL, CH]])
                        mm = pe.transpose(tp[n % 2][:, j * P:(j + 1) * P], src, ident[:, :])
                    mm.then_inc(tp_ready, 1)

            def turn_xT(g):
                pe.wait_ge(xrow_done, g + 1)
                for k in range(2):
                    n = TP_AT[("xT", g, k)]
                    tp_wait(pe, n)
                    for b in range(GB):
                        mm = pe.transpose(tp[n % 2][:, b * P:(b + 1) * P],
                                          xrow[:, g % 2, b, k * P:(k + 1) * P], ident[:, :])
                    mm.then_inc(tp_ready, 1)

            def wait_xT(g):
                pe.wait_ge(tp_free_dve, sum(not BY_ACT[k[0]] for k in TP[:TP_AT[("xT", g, 1)] + 1]))

            def logits(g):
                n = TP_AT[("logits", g, 0)]
                tp_wait(pe, n)
                wait_xT(g)
                if g == 0:
                    pe.wait_ge(wg_low, 1)
                for b in range(GB):
                    for k in range(2):
                        for j, (xt, wt) in enumerate(((xTh, wgh), (xTh, wgl), (xTl, wgh))):
                            mm = pe.matmul(tp[n % 2][:, b * E:(b + 1) * E], xt[:, g % 2, k, b * P:(b + 1) * P],
                                           wt[:, k, :], start=(k == 0 and j == 0), stop=(k == 1 and j == 2))
                mm.then_inc(tp_ready, 1)

            def places(g):
                n = TP_AT[("pos", g, 0)]
                tp_wait(pe, n)
                pe.wait_ge(onehot, g + 1)
                if g == 0:
                    pe.wait_ge(pool_consts, 3)
                o = tp[n % 2][:, 0:GB * E]
                pe.matmul(o, tri[:, :], oh[:, GB * g:GB * (g + 1), :].rearrange("p b e -> p (b e)"),
                          start=True, stop=False)
                pe.matmul(o, ones[:, :], acc[:, GB * g:GB * (g + 1), :].rearrange("p b e -> p (b e)"),
                          start=False, stop=True).then_inc(tp_ready, 1)

            def feed_forward(n):
                kind, blk, c = FU[n]
                bank, before = f_bank(n)
                if before is None:
                    for s in (CONV - 2, CONV - 1):
                        wait_products(pe, s, prods, zs_done)
                elif before >= 0:
                    pe.wait_ge(f_free, before + 1)
                w = weight_set(blk)
                i = w % 2
                if kind == "gu":
                    if c == 0:
                        if blk < 8:
                            wait_xT(blk // 2)
                        else:
                            pe.wait_ge(tp_free_dve, sum(not BY_ACT[k[0]] for k in TP[:TP_AT[("xe", blk - 8, 0)] + 1]))
                        pe.wait_ge(w_low_dve, 2 * w + 1)
                        pe.wait_ge(w_low_pool, w + 1)
                    place = (blk // 2) % 2 if blk < 8 else blk % 2
                    first = (blk % 2) * 256 if blk < 8 else 0
                    for m in range(2):
                        for k in range(2):
                            col = (m * 2 + k) * HID + HC[c]
                            for j, (wt, xt) in enumerate(((wh_gu, xTh), (wl_gu, xTh), (wh_gu, xTl))):
                                mm = pe.matmul(bank[:, m * 256:(m + 1) * 256], wt[:, i, col:col + P],
                                               xt[:, place, k, first:first + 256],
                                               start=(k == 0 and j == 0), stop=(k == 1 and j == 2))
                    mm.then_inc(f_ready, 1)
                else:
                    pe.wait_ge(h_high, GU_NUM[("gu", blk, 2)] + 1)
                    pe.wait_ge(h_low, GU_NUM[("gu", blk, 2)] + 1)
                    pe.wait_ge(w_low_dve, 2 * w + 2)
                    for t in range(2):
                        for c in range(3):
                            for j, (ht, wt) in enumerate(((hTh, wh_d), (hTl, wh_d), (hTh, wl_d))):
                                mm = pe.matmul(bank[:, t * L:(t + 1) * L], ht[:, blk % 2, c, t * P:(t + 1) * P],
                                               wt[:, i, c * L:(c + 1) * L],
                                               start=(c == 0 and j == 0), stop=(c == 2 and j == 2))
                    mm.then_inc(f_ready, 1)

            def turn_xe(e):
                n = TP_AT[("xe", e, 0)]
                tp_wait(pe, n)
                pe.wait_ge(xe_in[e % XRING], 16 * (e // XRING + 1))
                for k in range(2):
                    for t in range(2):
                        mm = pe.transpose(tp[n % 2][:, k * CAP + t * P:k * CAP + (t + 1) * P],
                                          xe[:, e % XRING, t, k * P:(k + 1) * P], ident[:, :])
                mm.then_inc(tp_ready, 1)

            pe.wait_ge(pool_consts, 1)
            convolve(0)
            turn_q(0)
            for s in range(SLOTS):
                if 1 <= s < CONV:
                    convolve(s)
                if s >= F0_SLOT:
                    feed_forward(s - F0_SLOT)
                for step, work in (("residual", turn_r), ("turn_q", turn_q), ("turn_xT", turn_xT),
                                   ("logits", logits), ("places", places)):
                    if due(step, s) >= 0:
                        work(due(step, s))
            turn_xe(0)
            for n in range(SHARED_USES, len(FU)):
                kind, blk, c = FU[n]
                feed_forward(n)
                if kind == "gu" and c == 1 and blk + 1 < 16:
                    turn_xe(blk + 1 - 8)


def lay_out(a):
    import numpy as np
    ctx = np.asarray(a["ctx_2048"])
    c = ctx.reshape(NG, GB, H, DH, BLK, P)[..., ::-1].transpose(0, 5, 2, 3, 4, 1)
    c = np.ascontiguousarray(c).reshape(NG, P, H, DH * PL)
    c = np.concatenate([c, c[..., :4 * PL]], axis=3)
    k = np.pad(np.asarray(a["L0_xattn_ssm_kernel"]), ((0, 0), (P - 1, 0)))
    f = lambda n: np.ascontiguousarray(np.asarray(a[n]))
    return {
        "x": f("x"), "ctxt": c.reshape(NG, P, H * CW), "kpad": np.ascontiguousarray(k),
        "skip_d": f("L0_xattn_D"), "g_x": f("g_xattn"), "g_f": f("g_ffn"), "wg": f("L0_ffn_Wg"),
        "w1": f("L0_ffn_W1"), "w3": f("L0_ffn_W3"), "w2": f("L0_ffn_W2"),
        "sw1": f("L0_ffn_sw1"), "sw3": f("L0_ffn_sw3"), "sw2": f("L0_ffn_sw2"),
    }


def kernel(**inputs):
    import concourse.bacc as bacc
    from concourse.bass_utils import run_bass_kernel_spmd

    nc = bacc.Bacc("TRN2", target_bir_lowering=False, num_devices=1)
    arrays = lay_out(inputs)
    args = [nc.dram_tensor(name, v.shape, F32, kind="ExternalInput").ap() for name, v in arrays.items()]
    out = nc.dram_tensor("out", (B, CH, L), F32, kind="ExternalOutput").ap()
    build(nc, *args, out)
    r = run_bass_kernel_spmd(nc, [arrays], core_ids=[0])
    return r.results[0]["out"]
```
